# Optimizing a Trainium2 kernel written in Bass

```python
import numpy as np
import jax
import jax.numpy as jnp

def _softmax(x, axis=-1):
    return jax.nn.softmax(x, axis=axis)

def _gelu(x):
    return jax.nn.gelu(x, approximate=True)

def _silu(x):
    return jax.nn.silu(x)

def _sigmoid(x):
    return jax.nn.sigmoid(x)

def _layernorm(x, axis=-1, eps=1e-05):
    m = jnp.mean(x, axis=axis, keepdims=True)
    v = jnp.var(x, axis=axis, keepdims=True)
    return (x - m) / jnp.sqrt(v + eps)

def _scatter_add(tgt, idx, src, axis=0):
    return tgt.at[idx].add(src)

def _segment_sum(src, seg, n):
    return jax.ops.segment_sum(src, seg, n)
kernel_name = 'mk_prb_d1_jaxref_r4_ebd07c'

def setup_inputs(seed: int=0):
    np.random.seed(seed)
    _w = jnp.asarray

    def _L0_attn_setup():
        import jax, jax.numpy as jnp
        import numpy as np
        D = 256
        H = 8
        NUM_LEVELS = 3
        CHUNK0 = 128
        OVERLAP = 64

        def _mha(x, Win, bin_, Wout, bout):
            B, T, _ = x.shape
            dh = D // H
            qkv = x @ Win.T + bin_
            q, k, v = jnp.split(qkv, 3, axis=-1)
            q = q.reshape(B, T, H, dh)
            k = k.reshape(B, T, H, dh)
            v = v.reshape(B, T, H, dh)
            scale = 1.0 / jnp.sqrt(jnp.asarray(dh, x.dtype))
            scores = jnp.einsum('bqhd,bkhd->bhqk', q, k) * scale
            attn = jax.nn.softmax(scores, axis=-1)
            out = jnp.einsum('bhqk,bkhd->bqhd', attn, v).reshape(B, T, D)
            return out @ Wout.T + bout

        def _forward(x, params):
            B, L, _ = x.shape
            chunk = min(CHUNK0, L)
            cur = x
            for level in range(NUM_LEVELS):
                stride = chunk - OVERLAP
                outs = [_mha(cur[:, i:min(i + chunk, L)], *params[level]) for i in range(0, L, stride)]
                cur = jnp.concatenate(outs, axis=1)[:, :L]
                chunk *= 2
            return cur
        key = jax.random.key(seed)
        ks = jax.random.split(key, 1 + 4 * NUM_LEVELS)
        inp = {'x': jax.random.normal(ks[0], (4, 2048, D), dtype=jnp.float32)}
        for l in range(NUM_LEVELS):
            k0, k1, k2, k3 = ks[1 + 4 * l:5 + 4 * l]
            inp[f'Win{l}'] = jax.random.normal(k0, (3 * D, D), dtype=jnp.float32) * 0.02
            inp[f'bin{l}'] = jax.random.normal(k1, (3 * D,), dtype=jnp.float32) * 0.02
            inp[f'Wout{l}'] = jax.random.normal(k2, (D, D), dtype=jnp.float32) * 0.02
            inp[f'bout{l}'] = jax.random.normal(k3, (D,), dtype=jnp.float32) * 0.02
        return inp
    _L0_attn_in = _L0_attn_setup()

    def _L0_ffn_setup():
        import jax, jax.numpy as jnp
        import numpy as np
        THRESH_FACTOR = 0.7

        def ternary_quantize(w):
            delta = THRESH_FACTOR * jnp.mean(jnp.abs(w))
            return jnp.where(w > delta, 1.0, jnp.where(w < -delta, -1.0, 0.0)).astype(w.dtype)
        key = jax.random.key(seed)
        k1, k2, k3 = jax.random.split(key, 3)
        B, S, D_IN, D_OUT = (8, 1024, 256, 256)
        inp = {'input': jax.random.normal(k1, (B, S, D_IN), dtype=jnp.float32), 'weight': jax.random.normal(k2, (D_OUT, D_IN), dtype=jnp.float32) * (1.0 / np.sqrt(D_IN)), 'alpha': jnp.ones((1,), dtype=jnp.float32), 'bias': jax.random.normal(k3, (D_OUT,), dtype=jnp.float32) * (1.0 / np.sqrt(D_IN))}
        return inp
    _L0_ffn_in = _L0_ffn_setup()
    _d = {'L0_attn_x': _L0_attn_in['x'], 'L0_attn_Win0': _L0_attn_in['Win0'], 'L0_attn_bin0': _L0_attn_in['bin0'], 'L0_attn_Wout0': _L0_attn_in['Wout0'], 'L0_attn_bout0': _L0_attn_in['bout0'], 'L0_attn_Win1': _L0_attn_in['Win1'], 'L0_attn_bin1': _L0_attn_in['bin1'], 'L0_attn_Wout1': _L0_attn_in['Wout1'], 'L0_attn_bout1': _L0_attn_in['bout1'], 'L0_attn_Win2': _L0_attn_in['Win2'], 'L0_attn_bin2': _L0_attn_in['bin2'], 'L0_attn_Wout2': _L0_attn_in['Wout2'], 'L0_attn_bout2': _L0_attn_in['bout2'], 'L0_ffn_weight': _L0_ffn_in['weight'], 'L0_ffn_alpha': _L0_ffn_in['alpha'], 'L0_ffn_bias': _L0_ffn_in['bias']}
    _x0 = _d['L0_attn_x']
    _d['L0_attn_x'] = jax.random.normal(jax.random.fold_in(jax.random.key(seed), 1), (2, 2048, 256), dtype=_x0.dtype)
    del _x0
    return _d

def reference(L0_attn_x, L0_attn_Win0, L0_attn_bin0, L0_attn_Wout0, L0_attn_bout0, L0_attn_Win1, L0_attn_bin1, L0_attn_Wout1, L0_attn_bout1, L0_attn_Win2, L0_attn_bin2, L0_attn_Wout2, L0_attn_bout2, L0_ffn_weight, L0_ffn_alpha, L0_ffn_bias):

    def _L0_attn_ref(x, Win0, bin0, Wout0, bout0, Win1, bin1, Wout1, bout1, Win2, bin2, Wout2, bout2):
        import jax, jax.numpy as jnp
        import numpy as np
        D = 256
        H = 8
        NUM_LEVELS = 3
        CHUNK0 = 128
        OVERLAP = 64

        def _mha(x, Win, bin_, Wout, bout):
            B, T, _ = x.shape
            dh = D // H
            qkv = x @ Win.T + bin_
            q, k, v = jnp.split(qkv, 3, axis=-1)
            q = q.reshape(B, T, H, dh)
            k = k.reshape(B, T, H, dh)
            v = v.reshape(B, T, H, dh)
            scale = 1.0 / jnp.sqrt(jnp.asarray(dh, x.dtype))
            scores = jnp.einsum('bqhd,bkhd->bhqk', q, k) * scale
            attn = jax.nn.softmax(scores, axis=-1)
            out = jnp.einsum('bhqk,bkhd->bqhd', attn, v).reshape(B, T, D)
            return out @ Wout.T + bout

        def _forward(x, params):
            B, L, _ = x.shape
            chunk = min(CHUNK0, L)
            cur = x
            for level in range(NUM_LEVELS):
                stride = chunk - OVERLAP
                outs = [_mha(cur[:, i:min(i + chunk, L)], *params[level]) for i in range(0, L, stride)]
                cur = jnp.concatenate(outs, axis=1)[:, :L]
                chunk *= 2
            return cur
        params = [(Win0, bin0, Wout0, bout0), (Win1, bin1, Wout1, bout1), (Win2, bin2, Wout2, bout2)]
        return _forward(x, params)

    def _L0_ffn_ref(input, weight, alpha, bias):
        import jax, jax.numpy as jnp
        import numpy as np
        THRESH_FACTOR = 0.7

        def ternary_quantize(w):
            delta = THRESH_FACTOR * jnp.mean(jnp.abs(w))
            return jnp.where(w > delta, 1.0, jnp.where(w < -delta, -1.0, 0.0)).astype(w.dtype)
        w_ternary = ternary_quantize(weight)
        w_eff = w_ternary * alpha
        out = jnp.einsum('bsd,od->bso', input, w_eff) + bias
        return out
    x = L0_attn_x
    xn = _layernorm(x, axis=-1)
    x = x + _L0_attn_ref(xn, L0_attn_Win0, L0_attn_bin0, L0_attn_Wout0, L0_attn_bout0, L0_attn_Win1, L0_attn_bin1, L0_attn_Wout1, L0_attn_bout1, L0_attn_Win2, L0_attn_bin2, L0_attn_Wout2, L0_attn_bout2) + _L0_ffn_ref(xn, L0_ffn_weight, L0_ffn_alpha, L0_ffn_bias)
    return x

_drawn_inputs = setup_inputs


def setup_inputs(seed=0):
    import zlib

    import numpy as np

    out = dict(_drawn_inputs(seed))
    spreads = {}
    factors = {'L0_attn_Win0': 8.0,
     'L0_attn_bin0': 8.0,
     'L0_attn_Wout0': 8.0,
     'L0_attn_bout0': 8.0,
     'L0_attn_Win1': 8.0,
     'L0_attn_bin1': 8.0,
     'L0_attn_Wout1': 8.0,
     'L0_attn_bout1': 8.0,
     'L0_attn_Win2': 8.0,
     'L0_attn_bin2': 8.0,
     'L0_attn_Wout2': 8.0,
     'L0_attn_bout2': 200.0,
     'L0_ffn_bias': 200.0}
    for name, (base, spread) in spreads.items():
        noise = np.random.default_rng([zlib.crc32(name.encode()), seed]).standard_normal(out[name].shape)
        drawn = base * np.exp(spread * noise) if base else spread * noise
        out[name] = jnp.asarray(drawn.astype(out[name].dtype))
    for name, factor in factors.items():
        out[name] = (out[name] * factor).astype(out[name].dtype)
    return out
```

```python
from contextlib import ExitStack

import concourse.bass as bass
from concourse import mybir

ALU = mybir.AluOpType
ACT = mybir.ActivationFunctionType
AX_X = mybir.AxisListType.X
F32 = mybir.dt.float32
F16 = mybir.dt.float16
I32 = mybir.dt.int32
ds = bass.ds

P = 128
B = 2
L = 2048
D = 256
O3 = 3 * D
DH = 32
IT = D // P
OVERLAP = 64
QK_TILES = 2 * D // P
BLK = 256
STEP_COLS = 2048
NBUF = 4
PSLOTS = 8
EXPONENT = 0x7F800000
SHIFT_ROW = 96
SHIFT_HI, SHIFT_LO = 2.0 ** 14, 2.0 ** 3
ACC_BOUND = 2.0 ** 12
ROW_BOUND = 2.0 ** 10
NORM_BOUND = 16.0
EPS = 1e-5


class Level:

    def __init__(self, n, chunk, chunks, in_rows, heads, batches):
        self.n, self.T = n, chunk
        self.stride = chunk - OVERLAP
        self.chunks = chunks
        self.in_rows = in_rows
        self.heads, self.batches = heads, batches
        self.steps = chunks * (B // batches) * (8 // heads)
        self.units = STEP_COLS // 128 * chunk // 512
        self.per_burst = {0: 1, 1: 4, 2: 4}[n]
        self.bursts = self.units // self.per_burst
        self.mx_cols = 16 // self.units

    def query_unit(self, u):
        if self.n == 2:
            return [(0, u * 128, (u // 4) * 512, 512)]
        if self.n == 1:
            return [(qt * 256, u * 256 + qt * 128, u * 256, 256) for qt in range(2)]
        return [(j * 128, (4 * u + j) * 128, (4 * u + j) * 128, 128) for j in range(4)]

    def key_unit(self, u):
        if self.n == 2:
            h, kt = u % 4, u // 4
            return [(0, h * 512 + kt * 128, h * 512, 512)]
        if self.n == 1:
            return [(kt * 256, u * 256 + kt * 128, u * 256, 256) for kt in range(2)]
        return [(j * 128, (4 * u + j) * 128, (4 * u + j) * 128, 128) for j in range(4)]

    def shift_half(self, u):
        if self.n == 2:
            return 1
        return 2 * u // self.units

    def value_products(self, g):
        if self.n == 2:
            return [(q, 4 * g + q, 0, 512, g * 128 + q * DH, 0, g == 0, g == 3) for q in range(4)]
        if self.n == 1:
            return [(q, 4 * g + q, kt * 256, 256, kt * 256 + g * 128 + q * DH, g * 256, kt == 0, kt == 1)
                    for kt in range(2) for q in range(4)]
        return [(q, g, q * 128, 128, (g // 2) * 256 + (g % 2) * 128 + q * DH, g * 128, True, True)
                for q in range(4)]

    def sum_products(self, g):
        if self.n == 2:
            return [(q, 4 * g + q, j * 128, j, g == 0 and j == 0, g == 3 and j == 3)
                    for j in range(4) for q in range(4)]
        if self.n == 1:
            return [(q, 4 * g + q, kt * 256 + qb * 128, 2 * g + qb, g + kt + qb == 0, g + kt + qb == 3)
                    for kt in range(2) for qb in range(2) for q in range(4)]
        return [(q, g, q * 128, g, g == 0, g == 3) for q in range(4)]

    def tokens(self, has_c=True, has_b=True, has_n=True):
        out, s = [], 0
        if has_n:
            out.append(("R", 0))
        flushed, vs = 0, 0
        for u in range(self.units):
            if has_c:
                out.append(("T", u))
            if has_n:
                if u == 1:
                    out.append(("O", 0))
                if u == 2:
                    out.append(("N", 0))
                if u == min(5, self.units - 1):
                    out.append(("H", 0))
            if has_b:
                while flushed < 2 and s >= (flushed + 1) * self.units // 2 + (1 if flushed == 0 else 0):
                    out.append(("M", flushed))
                    flushed += 1
                while s < self.units and s * 3 < (u + 1) * 4:
                    out.append(("S", s))
                    s += 1
            if has_c:
                while vs < self.bursts and u >= (vs + 1) * self.per_burst + 1:
                    out.append(("V", vs))
                    vs += 1
        if has_b:
            while flushed < 2:
                out.append(("M", flushed))
                flushed += 1
        if has_c:
            out += [("V", g) for g in range(vs, self.bursts)]
        return out


LEVELS = [Level(0, 128, 13, 1024, 8, 2), Level(1, 256, 8, 1664, 8, 1), Level(2, 512, 4, 2048, 4, 1)]


def before(values, n):
    return sum(values[:n])


def build(nc, t, out):
    x_d = t["L0_attn_x"].rearrange("b l d -> (b l) d")
    out_d = out.rearrange("b l d -> (b l) d")
    rows_of = [B * lv.in_rows for lv in LEVELS]
    qk_d = [nc.dram_tensor(f"qk_scratch{n}", (2, QK_TILES, P, r), F16, kind="Internal").ap()
            for n, r in enumerate(rows_of)]
    v_d = [nc.dram_tensor(f"v_scratch{n}", (r, D), F32, kind="Internal").ap() for n, r in enumerate(rows_of)]

    ctx = ExitStack()
    with ctx:
        def sb(name, shape, dt=F32):
            return ctx.enter_context(nc.sbuf_tensor(name, shape, dt))

        def sem(name):
            return ctx.enter_context(nc.semaphore(name))

        xT = [sb(f"xT{n}", [P, 2, IT, B * L], F16) for n in range(3)]
        wT = [sb(f"wT{n}", [P, 2, IT, O3], F16) for n in range(3)]
        woT = sb("woT", [P, 2, IT, D], F16)
        ternT = sb("ternT", [P, IT, D], F16)
        q_pack = [sb(f"q_pack{i}", [P, STEP_COLS], F16) for i in range(NBUF)]
        k_pack = [sb(f"k_pack{i}", [P, STEP_COLS], F16) for i in range(NBUF)]
        v_pack = [sb(f"v_pack{i}", [P, 512]) for i in range(NBUF)]
        probs = sb("probs", [P, PSLOTS, 512])
        qk_stage = sb("qk_stage", [P, 2, QK_TILES, BLK], F16)
        v_stage = sb("v_stage", [P, 2, D])
        row_max = sb("row_max", [P, 16])
        shift = [sb(f"shift{h}", [8, 2, 128], F16) for h in range(2)]
        shift_big = sb("shift_big", [8, 128])
        recips = sb("recips", [P, 128])
        attn = sb("attn", [P, 512])
        attn_n = sb("attn_n", [P, 512])
        ident = sb("ident", [P, P])
        ones = sb("ones", [P, P])
        sum_sel = sb("sum_sel", [P, 4, DH])
        spread_sel = sb("spread_sel", [P, 4, P])
        bias_col = sb("bias_col", [P, 3, QK_TILES])
        bias_v = sb("bias_v", [P, 3, D])
        sc = sb("sc", [P, 3, 16])
        fin = sb("fin", [P, 8])
        row_add = sb("row_add", [P, D])
        alpha = sb("alpha", [P, 1])
        stats = sb("stats", [P, 16, 6])
        mv = sb("mv", [P, 16, 2])
        rs = sb("rs", [P, 6, 16])
        prep2 = xT[2][:, :, :, :].rearrange("p a b c -> p (a b c)").bitcast(F32)
        prep1 = xT[1][:, :, :, :].rearrange("p a b c -> p (a b c)").bitcast(F32)
        win_n = [prep2[:, n * 1536:(n + 1) * 1536].rearrange("p (a d) -> p a d", a=6) for n in range(3)]
        wout_n = [prep2[:, 4608 + n * 512:4608 + (n + 1) * 512].rearrange("p (a d) -> p a d", a=2) for n in range(3)]
        w_eff = prep2[:, 6144:7680].rearrange("p (a o) -> p a o", a=2)
        tern_n = prep2[:, 7680:8192].rearrange("p (a d) -> p a d", a=2)
        win_t = [prep1[:, n * 1536:(n + 1) * 1536].rearrange("p (a o) -> p a o", a=2) for n in range(3)]
        w_sq = prep1[:, 4608:6144].rearrange("p (a o) -> p a o", a=2)
        b_row = prep1[:, 6144:6912]
        b_sq = prep1[:, 6912:7680]
        bout_bc = prep1[:, 7680:7936].rearrange("p (a m) -> p a m", a=2)
        bin_row = [q_pack[n][:, :].bitcast(F32)[:, 0:O3] for n in range(3)]
        bin_col = sb("bin_col", [P, 3, QK_TILES])
        bout_col = sb("bout_col", [P, 3, IT])
        bout2_row = sb("bout2_row", [P, D])
        x_ln = probs[:, :, :].rearrange("p a (t d) -> p (a t) d", d=D)
        x_fin = [probs[:, i, 0:D] for i in range(4)]
        y_fin = [probs[:, i, D:2 * D] for i in range(4)]
        o_fin = [probs[:, 4 + i, 0:D] for i in range(4)]

        ps = ctx.enter_context(nc.psum_tensor("ps", [P, 8, 512], F32))
        O_BANK, D_BANK, SPREAD_BANK, SHIFT_BANK = 4, 5, 6, 7

        win_in = [sem(f"win_in{n}") for n in range(3)]
        small_in = sem("small_in")
        consts_ready = sem("consts_ready")
        pool_chain = sem("pool_chain")
        dve_chain = sem("dve_chain")
        wt_turned = sem("wt_turned")
        wt_copied = sem("wt_copied")
        bout_spread = sem("bout_spread")
        fused = sem("fused")
        fused_copied = sem("fused_copied")
        biased = sem("biased")
        squared = sem("squared")
        sq_summed = sem("sq_summed")
        roots_wanted = sem("roots_wanted")
        roots = sem("roots")
        w_split = sem("w_split")
        last_ready = sem("last_ready")
        last_summed = sem("last_summed")
        last_turned = sem("last_turned")
        x_in = sem("x_in")
        ln_var = sem("ln_var")
        ln_root = sem("ln_root")
        ln_scale = sem("ln_scale")
        ln_applied = sem("ln_applied")
        ln_turned = sem("ln_turned")
        ln_hi = sem("ln_hi")
        ln_lo = sem("ln_lo")
        lin_done = sem("lin_done")
        qk_hi = sem("qk_hi")
        qk_lo = sem("qk_lo")
        v_out = sem("v_out")
        qk_stored = sem("qk_stored")
        v_stored = sem("v_stored")
        packed = [sem(f"packed{i}") for i in range(NBUF)]
        pack_free = sem("pack_free")
        scored = sem("scored")
        maxed = sem("maxed")
        turned = sem("turned")
        split_hi = sem("split_hi")
        split = sem("split")
        shift_in = [sem(f"shift_in{h}") for h in range(2)]
        scored_t = sem("scored_t")
        exped = sem("exped")
        bursts = sem("bursts")
        recip_done = sem("recip_done")
        o_copied = sem("o_copied")
        spread = sem("spread")
        normed = sem("normed")
        x_hi = sem("x_hi")
        x_lo = sem("x_lo")
        xf_in = [sem(f"xf_in{i}") for i in range(4)]
        row_added = sem("row_added")
        fin_mm = sem("fin_mm")
        fin_y = sem("fin_y")
        fin_acc = sem("fin_acc")
        fin_o = sem("fin_o")
        stored = [sem(f"stored{i}") for i in range(4)]

        block = ctx.enter_context(nc.Block())

        steps = [lv.steps for lv in LEVELS]
        lin_blocks = [r // BLK for r in rows_of]
        GX, U2, SV, RT, RV, GW, SX, GQ, GXN, ESC, TMP, TMP2 = range(12)
        SMALL_DMAS = 13

        def packed_base(n, i):
            return sum(16 * per_step_dmas(m) * len(range(i, LEVELS[m].steps, NBUF)) for m in range(n))

        def per_step_dmas(n):
            return 13 if n == 0 else 7

        def slots(n, emit, eng):
            S = steps[n]
            turns = (S - NBUF) // NBUF
            emit(-1, 3)
            emit(0, 0)
            with eng.Fori(0, turns) as i:
                for u in range(NBUF):
                    emit(i * NBUF + (1 + u), (1 + u) % NBUF)
            for s in range(1 + NBUF * turns, S + 1):
                emit(s, s % NBUF)

        def parts(n, s):
            if not isinstance(s, int):
                return True, True, True
            return 0 <= s < steps[n], s + 1 < steps[n], s >= 1

        def src_row(lv, s, u):
            if lv.n == 0:
                return s * lv.stride
            if lv.n == 1:
                return (s - u % 2) * (lv.stride // 2) + (u % 2) * lv.in_rows
            return (s - u % 4) * (lv.stride // 4) + (u % 4 // 2) * lv.in_rows

        def dst_row(lv, s, u):
            if lv.n == 0:
                return s * lv.T
            if lv.n == 1:
                return (s - u % 2) * (lv.T // 2) + (u % 2) * L
            return (s - u % 4) * (lv.T // 4) + (u % 4 // 2) * L

        OUT_ROWS0 = LEVELS[1].in_rows

        def wait(eng, s, v):
            eng.wait_ge(s, v)

        def prob_slot(lv, u, unit):
            return (4 * (u % 2) + unit) if lv.n == 0 else unit % PSLOTS

        def out_slices(lv, s, u, hl):
            x = xT[(lv.n + 1) % 3] if lv.n < 2 else xT[1]
            r = dst_row(lv, s, u)
            if lv.n == 2:
                return [x[:, hl, u % 2, ds(r, 512)]], [attn_n[:, :]]
            if lv.n == 1:
                return [x[:, hl, :, ds(r, 256)]], [attn_n[:, :].rearrange("p (g q) -> p g q", g=2)]
            return ([x[:, hl, :, ds(r + b * OUT_ROWS0, 128)] for b in range(B)],
                    [attn_n[:, b * 256:(b + 1) * 256].rearrange("p (g q) -> p g q", g=2) for b in range(B)])

        @block.gpsimd
        def _(pool):
            n = 0

            def link(ins):
                nonlocal n
                n += 1
                ins.then_inc(pool_chain, 1)
                pool.wait_ge(pool_chain, n)

            link(pool.memset(ident[:, :], 0.0))
            link(pool.affine_select(out=ident[:, :], in_=ident[:, :], compare_op=ALU.not_equal, fill=1.0,
                                    base=0, pattern=[[-1, P]], channel_multiplier=1))
            link(pool.memset(ones[:, :], 1.0))
            link(pool.memset(sum_sel[:, :, :], 0.0))
            sel = sum_sel[:, :, :].rearrange("p a (b c) -> p a b c", b=4)
            link(pool.affine_select(out=sel, in_=sel, compare_op=ALU.not_equal, fill=1.0,
                                    base=0, pattern=[[1, 4], [-1, 4], [0, 8]], channel_multiplier=0))
            link(pool.memset(spread_sel[:, :, :], 0.0))
            sel = spread_sel[:, :, :].rearrange("p a (b c) -> p a b c", b=4)
            link(pool.affine_select(out=sel, in_=sel, compare_op=ALU.not_equal, fill=1.0,
                                    base=0, pattern=[[-8, 4], [-32, 4], [0, 32]], channel_multiplier=1))
            for i in range(NBUF):
                two = k_pack[i][SHIFT_ROW:SHIFT_ROW + 2, :]
                link(pool.memset(two, SHIFT_HI))
                link(pool.affine_select(out=two, in_=two, compare_op=ALU.not_equal, fill=SHIFT_LO,
                                        base=-1, pattern=[[0, STEP_COLS]], channel_multiplier=1))
            pool.sem_inc(consts_ready, 1)

            pool.sem_inc(x_lo, 1)

            def low_half(lv, s, u):
                g = before(steps, lv.n) + s
                pool.wait_ge(x_hi, g + 1)
                dst, src = out_slices(lv, s, u, 1)
                hi, _ = out_slices(lv, s, u, 0)
                for k, (d, h, a) in enumerate(zip(dst, hi, src)):
                    ins = pool.tensor_tensor(d, a, h, ALU.subtract)
                ins.then_inc(x_lo, 1)

            for lv in LEVELS:
                def emit(s, u, lv=lv):
                    if parts(lv.n, s)[2]:
                        low_half(lv, s - 1, (u - 1) % NBUF)
                slots(lv.n, emit, pool)

            pool.wait_ge(row_added, 1)
            with pool.Fori(0, B * L // P // 4) as i:
                for j in range(4):
                    pool.wait_ge(xf_in[j], i * 16 + 16)
                    pool.wait_ge(fin_o, i * 4 + (j + 1))
                    pool.tensor_tensor(y_fin[j], x_fin[j], row_add[:, :], ALU.add).then_inc(fin_y, 1)

        @block.sync
        def _(sp):
            sp.sem_inc(qk_stored, 16)
            sp.sem_inc(v_stored, 16)
            for j in range(4):
                sp.sem_inc(stored[j], 16)
            for n in range(3):
                sp.dma_start(win_n[n], t[f"L0_attn_Win{n}"].rearrange("(a p) d -> p a d", p=P)).then_inc(win_in[n], 16)
                sp.dma_start(wout_n[n], t[f"L0_attn_Wout{n}"].rearrange("(a p) d -> p a d", p=P)).then_inc(win_in[n], 16)
            with nc.allow_non_contiguous_dma(reason="short bias columns"):
                for n in range(3):
                    sp.dma_start(bin_col[:, n, :], t[f"L0_attn_bin{n}"][0:QK_TILES * P].rearrange("(a p) -> p a", p=P)).then_inc(small_in, 16)
                    sp.dma_start(bout_col[:, n, :], t[f"L0_attn_bout{n}"].rearrange("(a p) -> p a", p=P)).then_inc(small_in, 16)
            sp.dma_start(bout2_row[:, :], t["L0_attn_bout2"].rearrange("(o n) -> o n", o=1).broadcast_to((P, D))).then_inc(small_in, 16)
            sp.dma_start(row_add[:, :], t["L0_ffn_bias"].rearrange("(o n) -> o n", o=1).broadcast_to((P, D))).then_inc(small_in, 16)
            sp.dma_start(alpha[:, :], t["L0_ffn_alpha"].rearrange("(o n) -> o n", o=1).broadcast_to((P, 1))).then_inc(small_in, 16)
            sp.dma_start(tern_n, t["L0_ffn_weight"].rearrange("(a p) d -> p a d", p=P)).then_inc(small_in, 16)
            for n in range(3):
                sp.dma_start(bin_row[n], t[f"L0_attn_bin{n}"].rearrange("(o n) -> o n", o=1).broadcast_to((P, O3))).then_inc(small_in, 16)
            for b in range(B):
                if b:
                    sp.wait_ge(ln_turned, 8)
                sp.dma_start(x_ln, x_d[b * L:(b + 1) * L, :].rearrange("(a p) d -> p a d", p=P)).then_inc(x_in, 16)

            for lv in LEVELS:
                n, S = lv.n, lv.steps
                b0 = before(lin_blocks, n)
                with sp.Fori(0, lin_blocks[n]) as i:
                    sp.wait_ge(qk_lo, i * QK_TILES + (QK_TILES * (b0 + 1) + QK_TILES))
                    sp.dma_start(qk_d[n].rearrange("a o p r -> p (a o) r")[:, :, ds(i * BLK, BLK)],
                                 qk_stage[:, :, :, :].rearrange("p a o r -> p (a o) r")).then_inc(qk_stored, 16)
                    sp.wait_ge(v_out, i + (b0 + 2))
                    sp.dma_start(v_d[n].rearrange("(n a p) d -> n p a d", p=P, a=2)[ds(i, 1), :, :, :].rearrange("n p a d -> (n p) a d"),
                                 v_stage[:, :, :]).then_inc(v_stored, 16)
                sp.wait_ge(qk_stored, 16 * (b0 + lin_blocks[n] + 1))
                sp.wait_ge(v_stored, 16 * (b0 + lin_blocks[n] + 1))

                def load(s, u, lv=lv, n=n):
                    i = u % NBUF
                    sp.wait_ge(pack_free, s + (before(steps, n) + 1))
                    r = src_row(lv, s, u)
                    for b in range(lv.batches):
                        row = r + b * lv.in_rows
                        c0, c1 = b * lv.heads * lv.T, (b + 1) * lv.heads * lv.T
                        o0, on = (0, 2) if n < 2 else (u % 2, 1)
                        for part, pack, tile0 in (((0, 1, 0), q_pack[i], 0), ((0, 0, 1), k_pack[i], IT)):
                            for k, hl in enumerate(part):
                                src = qk_d[n][hl, tile0 + o0:tile0 + o0 + on, :, ds(row, lv.T)]
                                sp.dma_start(pack[k * DH:(k + 1) * DH, c0:c1].rearrange("p (h r) -> p h r", r=lv.T),
                                             src.rearrange("o (h p) r -> p (o h) r", p=DH)).then_inc(packed[i], 16)
                    if n == 0:
                        src = v_d[n].rearrange("(b r) d -> r b d", b=B)[ds(r, P), :, :]
                        dst = v_pack[i][:, :].rearrange("p (a d) -> p a d", a=2)
                    elif n == 1:
                        src = v_d[n][ds(r, lv.T), :].rearrange("(a p) d -> p a d", p=P)
                        dst = v_pack[i][:, :].rearrange("p (a d) -> p a d", a=2)
                    else:
                        src = v_d[n][ds(r, lv.T), (u % 2) * P:(u % 2 + 1) * P].rearrange("(a p) d -> p a d", p=P)
                        dst = v_pack[i][:, :].rearrange("p (a d) -> p a d", a=4)
                    sp.dma_start(dst, src).then_inc(packed[i], 16)

                def shifts(s, u, n=n):
                    for h in range(2):
                        sp.wait_ge(split, s * 2 + (2 * before(steps, n) + h + 2))
                        for hl in range(2):
                            sp.dma_start(q_pack[u % NBUF][SHIFT_ROW + hl:SHIFT_ROW + hl + 1, h * 1024:(h + 1) * 1024]
                                         .rearrange("o (c p) -> o c p", c=8), shift[h][:, hl, :]).then_inc(shift_in[h], 16)

                load(0, 0)
                load(1, 1)

                def emit(s, u, load=load, shifts=shifts, S=S):
                    if not isinstance(s, int) or s + 3 < S:
                        load(s + 3, (u + 3) % NBUF)
                    if parts(n, s)[1]:
                        shifts(s + 1, (u + 1) % NBUF)
                slots(n, emit, sp)

            sp.wait_ge(bursts, PSLOTS + sum(m.bursts * m.steps for m in LEVELS))
            for j in range(4):
                sp.dma_start(x_fin[j], x_d[j * P:(j + 1) * P, :]).then_inc(xf_in[j], 16)
            turns = B * L // P // 4
            with sp.Fori(0, turns - 1) as i:
                for j in range(4):
                    sp.wait_ge(fin_y, i * 4 + (j + 1))
                    sp.dma_start(x_fin[j], x_d[ds(i * (4 * P) + (4 + j) * P, P), :]).then_inc(xf_in[j], 16)
                    sp.wait_ge(fin_o, i * 4 + (j + 5))
                    sp.dma_start(out_d[ds(i * (4 * P) + j * P, P), :], o_fin[j]).then_inc(stored[j], 16)
            for j in range(4):
                sp.wait_ge(fin_o, 4 * turns + j + 1)
                sp.dma_start(out_d[(4 * turns - 4 + j) * P:(4 * turns - 3 + j) * P, :], o_fin[j]).then_inc(stored[j], 16)
            for j in range(4):
                sp.wait_ge(stored[j], 16 * (turns + 1))

        PRODUCTS = ((0, 0), (1, 0), (0, 1))

        @block.tensor
        def _(pe):
            pe.sem_inc(pack_free, NBUF)
            pe.sem_inc(bursts, PSLOTS)
            pe.wait_ge(consts_ready, 1)

            for n in range(3):
                pe.wait_ge(win_in[n], 32)
                if n:
                    pe.wait_ge(wt_copied, n)
                for it in range(IT):
                    for o in range(6):
                        m = pe.transpose(ps[:, 2 * it + o // 3, (o % 3) * P:(o % 3 + 1) * P],
                                         win_n[n][:, o, it * P:(it + 1) * P], ident[:, :])
                m.then_inc(wt_turned, 1)
            pe.wait_ge(wt_copied, 3)
            for n in range(3):
                if n:
                    if n > 1:
                        pe.wait_ge(fused_copied, n - 1)
                        pe.wait_ge(biased, n)
                    for it in range(IT):
                        for oh in range(2):
                            for jt in range(IT):
                                pe.matmul(ps[:, 2 * it + oh, 0:384], wout_n[n - 1][:, jt, it * P:(it + 1) * P],
                                          win_t[n][:, jt, oh * 384:(oh + 1) * 384], start=jt == 0, stop=jt == 1)
                    pe.wait_ge(bout_spread, n)
                    for oh in range(2):
                        for jt in range(IT):
                            pe.matmul(ps[:, 4 + oh, 0:384], bout_bc[:, jt, :],
                                      win_t[n][:, jt, oh * 384:(oh + 1) * 384], start=jt == 0, stop=jt == 1)
                    for o in range(QK_TILES):
                        for jt in range(IT):
                            m = pe.matmul(ps[:, 5, 400 + o:401 + o], win_t[n][:, jt, o * P:(o + 1) * P],
                                          bout_col[:, n - 1, jt:jt + 1], start=jt == 0, stop=jt == 1)
                    m.then_inc(fused, 1)
                pe.wait_ge(squared, n + 1)
                for oh in range(2):
                    for jt in range(IT):
                        m = pe.matmul(ps[:, 6 + oh, 0:384], ones[:, :], w_sq[:, jt, oh * 384:(oh + 1) * 384],
                                      start=jt == 0, stop=jt == 1)
                m.then_inc(sq_summed, 1)
            pe.wait_ge(last_ready, 1)
            pe.wait_ge(fused_copied, 2)
            m = pe.matmul(ps[:, 4, 0:2], ones[:, :], fin[:, 0:2], start=True, stop=True)
            m.then_inc(last_summed, 1)
            for it in range(IT):
                for a in range(2):
                    pe.transpose(ps[:, 0, it * D + a * P:it * D + (a + 1) * P],
                                 wout_n[2][:, a, it * P:(it + 1) * P], ident[:, :])
            pe.wait_ge(last_ready, 2)
            for it in range(IT):
                for a in range(2):
                    m = pe.transpose(ps[:, 1, it * D + a * P:it * D + (a + 1) * P],
                                     tern_n[:, a, it * P:(it + 1) * P], ident[:, :])
            m.then_inc(last_turned, 1)
            pe.wait_ge(w_split, 4)

            for b in range(B):
                for q in range(8):
                    g = 8 * b + q
                    pe.wait_ge(ln_applied, 16 * b + 2 * q + 2)
                    pe.wait_ge(ln_lo, g + 1)
                    for a in range(2):
                        for it in range(IT):
                            m = pe.transpose(ps[:, g % 4, it * 256 + a * P:it * 256 + (a + 1) * P],
                                             x_ln[:, 2 * q + a, it * P:(it + 1) * P], ident[:, :])
                    m.then_inc(ln_turned, 1)

            for lv in LEVELS:
                n = lv.n
                x, w = xT[n], wT[n]
                b0, g0 = before(lin_blocks, n), before(steps, n)
                u0 = sum(m.units * m.steps for m in LEVELS[:n])
                v0 = sum(m.bursts * m.steps for m in LEVELS[:n])

                def linear_block(blk, col):
                    for o in range(QK_TILES):
                        pe.wait_ge(qk_lo, blk * QK_TILES + (QK_TILES * b0 + o + 1))
                        for it in range(IT):
                            for k, (wh, xh) in enumerate(PRODUCTS):
                                m = pe.matmul(ps[:, o, 0:BLK], w[:, wh, it, o * P:(o + 1) * P],
                                              x[:, xh, it, ds(col, BLK)],
                                              start=it + k == 0, stop=it == 1 and k == 2)
                        m.then_inc(lin_done, 1)
                    pe.wait_ge(v_out, blk + (b0 + 1))
                    for a in range(2):
                        for it in range(IT):
                            for k, (wh, xh) in enumerate(PRODUCTS):
                                m = pe.matmul(ps[:, 4, a * D:(a + 1) * D], x[:, xh, it, ds(col + a * P, P)],
                                              w[:, wh, it, 2 * D:3 * D],
                                              start=it + k == 0, stop=it == 1 and k == 2)
                    m.then_inc(lin_done, 1)

                if n == 0:
                    pe.wait_ge(ln_lo, 16 + 4)
                    with pe.Fori(0, lin_blocks[0] // 2) as i:
                        linear_block(i, i * BLK)
                    with pe.Fori(0, lin_blocks[0] // 2) as i:
                        linear_block(i + lin_blocks[0] // 2, i * BLK + L)
                else:
                    pe.wait_ge(x_lo, g0 + 1)
                    with pe.Fori(0, lin_blocks[n]) as i:
                        linear_block(i, i * BLK)

                def emit(s, u, lv=lv, n=n, g0=g0, u0=u0, v0=v0):
                    has_c, has_b, has_n = parts(n, s)
                    qc, kc, vc = q_pack[u], k_pack[u], v_pack[u]
                    qb, kb = q_pack[(u + 1) % NBUF], k_pack[(u + 1) % NBUF]
                    for what, j in lv.tokens(has_c, has_b, has_n):
                        if what == "S":
                            if j == 0:
                                nb = (u + 1) % NBUF
                                pe.wait_ge(packed[nb], (s + 1 - nb) * (4 * per_step_dmas(n)) + (packed_base(n, nb) + 16 * per_step_dmas(n)))
                            pe.wait_ge(maxed, s * lv.units + (u0 + lv.units + j + 1))
                            for c, q, k, w_ in lv.query_unit(j):
                                m = pe.matmul(ps[:, j % 2, c:c + w_], qb[0:SHIFT_ROW, q:q + P], kb[0:SHIFT_ROW, k:k + w_],
                                              start=True, stop=True)
                            m.then_inc(scored, 1)
                        elif what == "M":
                            half = lv.units // 2
                            pe.wait_ge(maxed, s * lv.units + (u0 + lv.units + half * (j + 1) + 2))
                            pe.wait_ge(split, s * 2 + (2 * g0 + 2 + j + 1))
                            pe.transpose(ps[0:8, SHIFT_BANK, 0:P], row_max[:, 8 * j:8 * j + 8], ident[:, :]).then_inc(turned, 1)
                        elif what == "T":
                            if j == 0 or lv.shift_half(j) != lv.shift_half(j - 1):
                                for h in range(2 if lv.n == 2 else 1):
                                    hh = h if lv.n == 2 else lv.shift_half(j)
                                    pe.wait_ge(shift_in[hh], s * 32 + (32 * g0 + 32))
                            pe.wait_ge(exped, s * lv.units + (u0 + j + 1))
                            for c, k, q, w_ in lv.key_unit(j):
                                m = pe.matmul(ps[:, 2 + j % 2, c:c + w_], kc[0:SHIFT_ROW + 2, k:k + P], qc[0:SHIFT_ROW + 2, q:q + w_],
                                              start=True, stop=True)
                            m.then_inc(scored_t, 1)
                        elif what == "V":
                            pe.wait_ge(exped, s * lv.units + (u0 + (j + 1) * lv.per_burst + 2))
                            if j == 0:
                                pe.wait_ge(o_copied, s + (g0 + 1))
                                pe.wait_ge(recip_done, s + (g0 + 1))
                            for quad, unit, c, w_, vcol, oc, first, last in lv.value_products(j):
                                p = probs[:, prob_slot(lv, u, unit), c:c + w_]
                                m = pe.matmul(ps[quad * DH:(quad + 1) * DH, O_BANK, oc:oc + w_], vc[:, vcol:vcol + DH], p,
                                              start=first, stop=last)
                            if j == lv.bursts - 1:
                                m.then_inc(pack_free, 1)
                            for quad, unit, c, slab, first, last in lv.sum_products(j):
                                p = probs[:, prob_slot(lv, u, unit), c:c + P]
                                m = pe.matmul(ps[quad * DH:(quad + 1) * DH, D_BANK, 0:P], sum_sel[:, slab, :], p,
                                              start=first, stop=last)
                            m.then_inc(bursts, 1)
                        elif what == "N":
                            pe.wait_ge(recip_done, s + (g0 + 1))
                            pe.wait_ge(normed, s + g0)
                            for j4 in range(4):
                                m = pe.matmul(ps[:, SPREAD_BANK, j4 * P:(j4 + 1) * P], spread_sel[:, j4, :], recips[:, :],
                                              start=True, stop=True)
                            m.then_inc(spread, 1)
                slots(n, emit, pe)

            pe.wait_ge(x_lo, before(steps, 3) + 1)
            with pe.Fori(0, B * L // P // 4) as i:
                for j in range(4):
                    col = i * (4 * P) + j * P
                    pe.wait_ge(fin_o, i * 4 + (j + 1))
                    for it in range(IT):
                        for k, (wh, xh) in enumerate(PRODUCTS):
                            pe.matmul(ps[:, j, 0:D], xT[1][:, xh, it, ds(col, P)], woT[:, wh, it, :],
                                      start=it + k == 0, stop=it == 1 and k == 2)
                    for it in range(IT):
                        for hl in range(2):
                            m = pe.matmul(ps[:, j, D:2 * D], xT[0][:, hl, it, ds(col, P)], ternT[:, it, :],
                                          start=it + hl == 0, stop=it + hl == 2)
                    m.then_inc(fin_mm, 1)

        @block.scalar
        def _(act):
            act.sem_inc(exped, 2)
            act.sem_inc(o_copied, 1)
            for n in range(3):
                act.wait_ge(wt_turned, n + 1)
                for it in range(IT):
                    for oh in range(2):
                        m = act.activation(win_t[n][:, it, oh * 384:(oh + 1) * 384], ps[:, 2 * it + oh, 0:384], ACT.Copy)
                m.then_inc(wt_copied, 1)
            for n in range(3):
                if n:
                    act.wait_ge(fused, n)
                    if n > 1:
                        act.wait_ge(w_split, n)
                    for it in range(IT):
                        for oh in range(2):
                            m = act.activation(w_eff[:, it, oh * 384:(oh + 1) * 384], ps[:, 2 * it + oh, 0:384], ACT.Copy)
                    m.then_inc(fused_copied, 1)
                act.wait_ge(roots_wanted, n + 1)
                act.activation(sc[:, n, RT:RT + 2], sc[:, n, U2:U2 + 2], ACT.Sqrt).then_inc(roots, 1)
            act.wait_ge(roots_wanted, 4)
            act.activation(fin[:, 3:4], fin[:, 2:3], ACT.Sqrt).then_inc(roots, 1)

            for b in range(B):
                act.wait_ge(ln_var, b + 1)
                act.activation(rs[:, 1, :], rs[:, 0, :], ACT.Sqrt).then_inc(ln_root, 1)
                act.wait_ge(ln_scale, b + 1)
                for q in range(9):
                    if q < 8:
                        for a in range(2):
                            k = 2 * q + a
                            act.activation(x_ln[:, k, :], x_ln[:, k, :], ACT.Identity, scale=rs[:, 4, k:k + 1],
                                           bias=rs[:, 5, k:k + 1]).then_inc(ln_applied, 1)
                    if q:
                        g = 8 * b + q - 1
                        act.wait_ge(ln_turned, g + 1)
                        act.activation(xT[0][:, 0, :, g * 256:(g + 1) * 256],
                                       ps[:, g % 4, :].rearrange("p (a r) -> p a r", a=IT), ACT.Copy).then_inc(ln_hi, 1)

            for lv in LEVELS:
                n = lv.n
                b0, g0 = before(lin_blocks, n), before(steps, n)
                u0 = sum(m.units * m.steps for m in LEVELS[:n])
                v0 = sum(m.bursts * m.steps for m in LEVELS[:n])
                with act.Fori(0, lin_blocks[n]) as i:
                    act.wait_ge(qk_stored, i * 16 + 16 * (b0 + 1))
                    for o in range(QK_TILES):
                        act.wait_ge(lin_done, i * (QK_TILES + 1) + ((QK_TILES + 1) * b0 + o + 1))
                        act.activation(qk_stage[:, 0, o, :], ps[:, o, 0:BLK], ACT.Identity,
                                       bias=bias_col[:, n, o:o + 1]).then_inc(qk_hi, 1)

                def emit(s, u, lv=lv, n=n, g0=g0, u0=u0, v0=v0):
                    for what, j in lv.tokens(*parts(n, s)):
                        if what == "T":
                            act.wait_ge(scored_t, s * lv.units + (u0 + j + 1))
                            act.wait_ge(bursts, s * lv.bursts + (PSLOTS + v0 + j // lv.per_burst + 1 - PSLOTS // lv.per_burst))
                            act.activation(probs[:, prob_slot(lv, u, j), :], ps[:, 2 + j % 2, :], ACT.Exp,
                                           scale=sc[:, n, ESC:ESC + 1]).then_inc(exped, 1)
                        elif what == "O":
                            act.wait_ge(bursts, s * lv.bursts + (PSLOTS + v0))
                            act.wait_ge(normed, s + g0)
                            act.activation(attn[:, :], ps[:, O_BANK, :], ACT.Copy).then_inc(o_copied, 1)
                        elif what == "H":
                            act.wait_ge(normed, s + (g0 + 1))
                            dst, src = out_slices(lv, s - 1, (u - 1) % NBUF, 0)
                            for d, a in zip(dst, src):
                                m = act.activation(d, a, ACT.Copy)
                            m.then_inc(x_hi, 1)
                slots(n, emit, act)

        @block.vector
        def _(dve):
            chained = 0

            def link(ins):
                nonlocal chained
                chained += 1
                ins.then_inc(dve_chain, 1)
                dve.wait_ge(dve_chain, chained)

            def power_of_two(to, of, bound):
                link(dve.reciprocal(to, of))
                link(dve.tensor_scalar(to, to, bound, None, ALU.mult))
                link(dve.tensor_scalar(to.bitcast(I32), to.bitcast(I32), EXPONENT, None, ALU.bitwise_and))

            dve.sem_inc(maxed, 2)
            dve.sem_inc(split, 1)
            dve.sem_inc(recip_done, 1)
            dve.sem_inc(normed, 1)
            dve.sem_inc(qk_lo, QK_TILES)
            dve.sem_inc(v_out, 1)
            dve.sem_inc(ln_lo, 4)
            dve.sem_inc(fin_o, 4)
            dve.wait_ge(consts_ready, 1)
            dve.wait_ge(small_in, 16 * SMALL_DMAS)

            for n in range(3):
                def col(k, w=1, n=n):
                    return sc[:, n, k:k + w]
                if n == 0:
                    w, brow, bcol = win_t[0], bin_row[0], bin_col[:, 0, :]
                    link(dve.memset(col(GX), 1.0))
                    dve.wait_ge(wt_copied, 1)
                else:
                    w, brow, bcol = w_eff, b_row, bin_col[:, n, :]
                    for jt in range(IT):
                        m = dve.tensor_scalar(bout_bc[:, jt, :], ones[:, :], bout_col[:, n - 1, jt:jt + 1], None, ALU.mult)
                    m.then_inc(bout_spread, 1)
                    link(dve.tensor_copy(col(GX), sc[:, n - 1, GXN:GXN + 1]))
                    dve.wait_ge(fused, n)
                    for oh in range(2):
                        dve.tensor_tensor(b_row[:, oh * 384:(oh + 1) * 384], ps[:, 4 + oh, 0:384],
                                          bin_row[n][:, oh * 384:(oh + 1) * 384], ALU.add)
                    link(dve.tensor_tensor(bcol, ps[:, 5, 400:400 + QK_TILES], bcol, ALU.add))
                    dve.wait_ge(fused_copied, n)
                for it in range(IT):
                    m = dve.tensor_tensor(w_sq[:, it, :], w[:, it, :], w[:, it, :], ALU.mult)
                m.then_inc(squared, 1)
                dve.sem_inc(biased, 1)
                link(dve.tensor_scalar(b_sq, brow, col(GX), None, ALU.mult))
                link(dve.tensor_tensor(b_sq, b_sq, b_sq, ALU.mult))
                dve.wait_ge(sq_summed, n + 1)
                r2 = (NORM_BOUND if n == 0 else ROW_BOUND) ** 2
                dve.scalar_tensor_tensor(out=b_sq[:, 0:384], in0=ps[:, 6, 0:384], scalar=r2, in1=b_sq[:, 0:384],
                                         op0=ALU.mult, op1=ALU.add)
                link(dve.scalar_tensor_tensor(out=b_sq[:, 384:768], in0=ps[:, 7, 0:384], scalar=r2, in1=b_sq[:, 384:768],
                                              op0=ALU.mult, op1=ALU.add))
                dve.reduce_max(col(U2), b_sq, AX_X)
                link(dve.reduce_sum(col(SV), b_sq[:, 2 * D:3 * D], AX_X))
                m = dve.tensor_scalar(col(U2, 2), col(U2, 2), 2.0, 1e-30, ALU.mult, ALU.add)
                m.then_inc(roots_wanted, 1)
                dve.wait_ge(roots, n + 1)
                power_of_two(col(GW), col(RT), ACC_BOUND)
                link(dve.tensor_tensor(col(TMP), col(RV), col(GW), ALU.mult))
                power_of_two(col(SX), col(TMP), ROW_BOUND)
                link(dve.tensor_tensor(col(GQ), col(GX), col(GW), ALU.mult))
                dve.tensor_tensor(col(GXN), col(GQ), col(SX), ALU.mult)
                link(dve.tensor_tensor(col(TMP), col(GQ), col(GQ), ALU.mult))
                link(dve.reciprocal(col(TMP2), col(TMP)))
                dve.tensor_scalar(col(ESC), col(TMP2), float(DH) ** -0.5, None, ALU.mult)
                dve.tensor_scalar(bias_col[:, n, :], bcol, col(GQ), None, ALU.mult)
                dve.tensor_scalar(bias_v[:, n, :], brow[:, 2 * D:3 * D], col(GXN), None, ALU.mult)
                for it in range(IT):
                    m = dve.tensor_scalar(wT[n][:, 0, it, :], w[:, it, :], col(GW), None, ALU.mult)
                link(m)
                for it in range(IT):
                    m = dve.scalar_tensor_tensor(out=wT[n][:, 1, it, :], in0=w[:, it, :], scalar=col(GW),
                                                 in1=wT[n][:, 0, it, :], op0=ALU.mult, op1=ALU.subtract)
                m.then_inc(w_split, 1)
                dve.wait_ge(w_split, n + 1)
            link(dve.tensor_tensor(w_sq[:, 0, 0:2 * D].rearrange("p (a d) -> p a d", a=2), wout_n[2], wout_n[2], ALU.mult))
            dve.reduce_sum(fin[:, 0:1], w_sq[:, 0, 0:2 * D], AX_X)
            dve.tensor_reduce(fin[:, 1:2], tern_n, mybir.AxisListType.XY, ALU.add, apply_absolute_value=True).then_inc(last_ready, 1)
            link(dve.tensor_tensor(row_add[:, :], row_add[:, :], bout2_row[:, :], ALU.add))
            dve.wait_ge(last_summed, 1)
            dve.tensor_scalar(fin[:, 2:3], ps[:, 4, 0:1], 1e-30, None, ALU.add).then_inc(roots_wanted, 1)
            dve.tensor_scalar(fin[:, 4:5], ps[:, 4, 1:2], 1.0 / (D * D), 0.7, ALU.mult, ALU.mult)
            link(dve.tensor_scalar(fin[:, 5:6], ps[:, 4, 1:2], 1.0 / (D * D), -0.7, ALU.mult, ALU.mult))
            sq = w_sq[:, 0, 0:2 * D].rearrange("p (a d) -> p a d", a=2)
            link(dve.tensor_scalar(sq, tern_n, fin[:, 5:6], None, ALU.is_lt))
            link(dve.tensor_scalar(tern_n, tern_n, fin[:, 4:5], None, ALU.is_gt))
            dve.tensor_tensor(tern_n, tern_n, sq, ALU.subtract).then_inc(last_ready, 1)
            dve.wait_ge(roots, 4)
            power_of_two(fin[:, 6:7], fin[:, 3:4], ACC_BOUND)
            link(dve.tensor_tensor(fin[:, 7:8], fin[:, 6:7], sc[:, 2, GXN:GXN + 1], ALU.mult))
            link(dve.reciprocal(fin[:, 7:8], fin[:, 7:8]))
            dve.wait_ge(last_turned, 1)
            wo = ps[:, 0, :].rearrange("p (a d) -> p a d", a=IT)
            link(dve.tensor_scalar(woT[:, 0, :, :], wo, fin[:, 6:7], None, ALU.mult))
            dve.scalar_tensor_tensor(out=woT[:, 1, :, :], in0=wo, scalar=fin[:, 6:7], in1=woT[:, 0, :, :],
                                     op0=ALU.mult, op1=ALU.subtract)
            dve.tensor_copy(ternT[:, :, :], ps[:, 1, :].rearrange("p (a d) -> p a d", a=IT)).then_inc(w_split, 1)
            dve.sem_inc(row_added, 1)

            for b in range(B):
                dve.wait_ge(x_in, 16 * (b + 1))
                for k in range(16):
                    m = dve.bn_stats(stats[:, k, :], x_ln[:, k, :])
                link(m)
                for k in range(16):
                    m = dve.bn_aggr(mv[:, k, :], stats[:, k, :])
                link(m)
                dve.tensor_scalar(rs[:, 0, :], mv[:, :, 1], EPS, None, ALU.add).then_inc(ln_var, 1)
                dve.wait_ge(ln_root, b + 1)
                link(dve.reciprocal(rs[:, 2, :], rs[:, 1, :]))
                link(dve.tensor_tensor(rs[:, 3, :], rs[:, 2, :], rs[:, 2, :], ALU.mult))
                link(dve.tensor_tensor(rs[:, 3, :], rs[:, 3, :], rs[:, 0, :], ALU.mult))
                link(dve.tensor_scalar(rs[:, 3, :], rs[:, 3, :], -0.5, 1.5, ALU.mult, ALU.add))
                link(dve.tensor_tensor(rs[:, 4, :], rs[:, 2, :], rs[:, 3, :], ALU.mult))
                dve.scalar_tensor_tensor(out=rs[:, 5, :], in0=mv[:, :, 0], scalar=-1.0, in1=rs[:, 4, :],
                                         op0=ALU.mult, op1=ALU.mult).then_inc(ln_scale, 1)
                for q in range(8):
                    g = 8 * b + q
                    dve.wait_ge(ln_hi, g + 1)
                    dve.tensor_tensor(xT[0][:, 1, :, g * 256:(g + 1) * 256], ps[:, g % 4, :].rearrange("p (a r) -> p a r", a=IT),
                                      xT[0][:, 0, :, g * 256:(g + 1) * 256], ALU.subtract).then_inc(ln_lo, 1)

            for lv in LEVELS:
                n = lv.n
                b0, g0 = before(lin_blocks, n), before(steps, n)
                u0 = sum(m.units * m.steps for m in LEVELS[:n])
                v0 = sum(m.bursts * m.steps for m in LEVELS[:n])
                with dve.Fori(0, lin_blocks[n]) as i:
                    dve.wait_ge(qk_stored, i * 16 + 16 * (b0 + 1))
                    for o in range(QK_TILES):
                        dve.wait_ge(qk_hi, i * QK_TILES + (QK_TILES * b0 + o + 1))
                        dve.scalar_tensor_tensor(out=qk_stage[:, 1, o, :], in0=ps[:, o, 0:BLK], scalar=bias_col[:, n, o:o + 1],
                                                 in1=qk_stage[:, 0, o, :], op0=ALU.add, op1=ALU.subtract).then_inc(qk_lo, 1)
                    dve.wait_ge(v_stored, i * 16 + 16 * (b0 + 1))
                    dve.wait_ge(lin_done, i * (QK_TILES + 1) + (QK_TILES + 1) * (b0 + 1))
                    for a in range(2):
                        m = dve.scalar_tensor_tensor(out=v_stage[:, a, :], in0=ps[:, 4, a * D:(a + 1) * D],
                                                     scalar=sc[:, n, SX:SX + 1], in1=bias_v[:, n, :],
                                                     op0=ALU.mult, op1=ALU.add)
                    m.then_inc(v_out, 1)

                def emit(s, u, lv=lv, n=n, g0=g0, u0=u0, v0=v0):
                    for what, j in lv.tokens(*parts(n, s)):
                        if what == "S":
                            dve.wait_ge(scored, s * lv.units + (u0 + lv.units + j + 1))
                            c = lv.mx_cols
                            dve.reduce_max(row_max[:, j * c:(j + 1) * c],
                                           ps[:, j % 2, :].rearrange("p (a k) -> p a k", a=c), AX_X).then_inc(maxed, 1)
                        elif what == "M":
                            dve.wait_ge(turned, s * 2 + (2 * g0 + 2 + j + 1))
                            if not isinstance(s, int) or s >= 0 or n:
                                dve.wait_ge(shift_in[j], s * 32 + (32 * g0 + 32))
                            dve.tensor_scalar(shift[j][:, 0, :], ps[0:8, SHIFT_BANK, 0:P], -1.0 / SHIFT_HI, None,
                                              ALU.mult).then_inc(split_hi, 1)
                            dve.wait_ge(split_hi, s * 4 + (4 * g0 + 4 + 2 * j + 1))
                            dve.tensor_scalar(shift_big[:, :], shift[j][:, 0, :], SHIFT_HI / SHIFT_LO, None,
                                              ALU.mult).then_inc(split_hi, 1)
                            dve.wait_ge(split_hi, s * 4 + (4 * g0 + 4 + 2 * j + 2))
                            dve.scalar_tensor_tensor(out=shift[j][:, 1, :], in0=ps[0:8, SHIFT_BANK, 0:P], scalar=-1.0 / SHIFT_LO,
                                                     in1=shift_big[:, :], op0=ALU.mult, op1=ALU.subtract).then_inc(split, 1)
                        elif what == "R":
                            dve.wait_ge(bursts, s * lv.bursts + (PSLOTS + v0))
                            dve.reciprocal(recips[:, :], ps[:, D_BANK, 0:P]).then_inc(recip_done, 1)
                        elif what == "N":
                            dve.wait_ge(spread, s + g0)
                            dve.wait_ge(o_copied, s + (g0 + 1))
                            dve.wait_ge(x_lo, s + g0)
                            dve.tensor_tensor(attn_n[:, :], attn[:, :], ps[:, SPREAD_BANK, :], ALU.mult).then_inc(normed, 1)
                slots(n, emit, dve)

            with dve.Fori(0, B * L // P // 4) as i:
                for j in range(4):
                    dve.wait_ge(fin_mm, i * 4 + (j + 1))
                    dve.wait_ge(fin_y, i * 4 + (j + 1))
                    dve.scalar_tensor_tensor(out=y_fin[j], in0=ps[:, j, 0:D], scalar=fin[:, 7:8], in1=y_fin[j],
                                             op0=ALU.mult, op1=ALU.add).then_inc(fin_acc, 1)
                    dve.wait_ge(fin_acc, i * 4 + (j + 1))
                    dve.wait_ge(stored[j], i * 16 + 16)
                    dve.scalar_tensor_tensor(out=o_fin[j], in0=ps[:, j, D:2 * D], scalar=alpha[:, 0:1], in1=y_fin[j],
                                             op0=ALU.mult, op1=ALU.add).then_inc(fin_o, 1)


_INS = (["L0_attn_x"] + [f"L0_attn_{w}{n}" for n in range(3) for w in ("Win", "bin", "Wout", "bout")]
        + ["L0_ffn_weight", "L0_ffn_alpha", "L0_ffn_bias"])


def kernel(**inputs):
    import numpy as _np
    import concourse.bacc as _bacc
    from concourse import mybir as _mybir
    from concourse.bass_utils import run_bass_kernel_spmd as _run

    nc = _bacc.Bacc("TRN2", target_bir_lowering=False, num_devices=1)
    arrays, handles = {}, {}
    for name in _INS:
        a = _np.ascontiguousarray(inputs[name])
        arrays[f"in_{name}"] = a
        handles[name] = nc.dram_tensor(f"in_{name}", a.shape, _mybir.dt.from_np(a.dtype), kind="ExternalInput").ap()
    out = nc.dram_tensor("out", (B, L, D), F32, kind="ExternalOutput").ap()
    build(nc, handles, out)
    r = _run(nc, [arrays], core_ids=[0])
    return r.results[0]["out"]
```

```python
from contextlib import ExitStack

import concourse.bass as bass
from concourse import mybir

ALU = mybir.AluOpType
ACT = mybir.ActivationFunctionType
AX_X = mybir.AxisListType.X
F32 = mybir.dt.float32
F16 = mybir.dt.float16
I32 = mybir.dt.int32
ds = bass.ds

P = 128
B = 2
L = 2048
D = 256
O3 = 3 * D
DH = 32
IT = D // P
OVERLAP = 64
QK_TILES = 2 * D // P
BLK = 256
STEP_COLS = 2048
NBUF = 4
PSLOTS = 8
EXPONENT = 0x7F800000
SHIFT_ROW = 96
SHIFT_HI, SHIFT_LO = 2.0 ** 14, 2.0 ** 3
ACC_BOUND = 2.0 ** 12
ROW_BOUND = 2.0 ** 10
NORM_BOUND = 16.0
EPS = 1e-5


class Level:

    def __init__(self, n, chunk, chunks, in_rows, heads, batches):
        self.n, self.T = n, chunk
        self.stride = chunk - OVERLAP
        self.chunks = chunks
        self.in_rows = in_rows
        self.heads, self.batches = heads, batches
        self.steps = chunks * (B // batches) * (8 // heads)
        self.units = STEP_COLS // 128 * chunk // 512
        self.per_burst = {0: 1, 1: 4, 2: 4}[n]
        self.bursts = self.units // self.per_burst
        self.mx_cols = 16 // self.units
        self.sum_bursts = {0: 4, 1: 2, 2: 2}[n]
        self.sums = {0: 0, 1: 8, 2: 8}[n]

    def query_unit(self, u):
        if self.n == 2:
            return [(0, u * 128, (u // 4) * 512, 512)]
        if self.n == 1:
            return [(qt * 256, u * 256 + qt * 128, u * 256, 256) for qt in range(2)]
        return [(j * 128, (4 * u + j) * 128, (4 * u + j) * 128, 128) for j in range(4)]

    def key_unit(self, u):
        if self.n == 2:
            h, kt = u % 4, u // 4
            return [(0, h * 512 + kt * 128, h * 512, 512)]
        if self.n == 1:
            return [(kt * 256, u * 256 + kt * 128, u * 256, 256) for kt in range(2)]
        return [(j * 128, (4 * u + j) * 128, (4 * u + j) * 128, 128) for j in range(4)]

    def shift_half(self, u):
        if self.n == 2:
            return u % 4 // 2
        return 2 * u // self.units

    def value_products(self, g):
        if self.n == 2:
            return [(q, 4 * g + q, 0, 512, g * 128 + q * DH, 0, g == 0, g == 3) for q in range(4)]
        if self.n == 1:
            return [(q, 4 * g + q, kt * 256, 256, kt * 256 + g * 128 + q * DH, g * 256, kt == 0, kt == 1)
                    for kt in range(2) for q in range(4)]
        return [(q, g, q * 128, 128, (g // 2) * 256 + (g % 2) * 128 + q * DH, g * 128, True, True)
                for q in range(4)]

    def ring(self, what, j):
        return [t for t in ORDER[self.n] if t[0] in "SM"].index((what, j))

    def last_scored(self, h):
        return self.ring("S", (h + 1) * self.units // 2 - 1) + 1

    def sum_jobs(self):
        if self.n == 2:
            return [(4 * (2 * m + 1) + q, (8 * m + q, 0, 512), (8 * m + 4 + q, 0, 512), (q, 0, 512))
                    for m in range(2) for q in range(4)]
        if self.n == 1:
            return [(u, (u, 0, 256), (u, 256, 256), (u // 2, 256 * (u % 2), 256)) for u in range(8)]
        return []

    def sum_products(self, g):
        if self.n == 2:
            return [(q, q, j * 128, j, g == 0 and j == 0, g == 1 and j == 3)
                    for j in range(4) for q in range(4)]
        if self.n == 1:
            return [(q, 2 * g + q // 2, 256 * (q % 2) + qb * 128, 2 * g + qb, g + qb == 0, g + qb == 2)
                    for qb in range(2) for q in range(4)]
        return [(q, g, q * 128, g, g == 0, g == 3) for q in range(4)]

    def tokens(self, has_c=True, has_b=True, has_n=True):
        return [t for t in ORDER[self.n] if (t[0] in "TVD" and has_c) or (t[0] in "SM" and has_b)
                or (t[0] in "WERONH" and has_n)]


def order(text):
    return [(w[0], int(w[1:] or 0)) for w in text.split()]


ORDER = {
    2: order("W S0 O S1 T0 S2 T1 S3 E S4 T2 R T3 S5 T4 S6 N T5 S7 T6 H S8 T7 V0 S9 M0 T8 S10 T9 V1 S11 T10 S12 D0 T11"
             " S13 T12 S14 T13 S15 V2 M1 T14 T15"),
    1: order("W S0 T0 O S1 T1 S2 T2 E S3 T3 R S4 T4 M0 N S5 T5 H V0 S6 T6 S7 T7 D0 M1"),
    0: order("W S0 T0 O S1 T1 E S2 R T2 M0 S3 T3 N M1 V0 D0 H V1 D1 V2 D2"),
}


LEVELS = [Level(0, 128, 13, 1024, 8, 2), Level(1, 256, 8, 1664, 8, 1), Level(2, 512, 4, 2048, 4, 1)]


def build(nc, t, out):
    x_d = t["L0_attn_x"].rearrange("b l d -> (b l) d")
    out_d = out.rearrange("b l d -> (b l) d")
    rows_of = [B * lv.in_rows for lv in LEVELS]
    qk_d = [nc.dram_tensor(f"qk_scratch{n}", (QK_TILES, P, 3, r), F16, kind="Internal").ap()
            for n, r in enumerate(rows_of)]
    v_d = [nc.dram_tensor(f"v_scratch{n}", (r, D), F32, kind="Internal").ap() for n, r in enumerate(rows_of)]

    ctx = ExitStack()
    with ctx:
        def sb(name, shape, dt=F32):
            return ctx.enter_context(nc.sbuf_tensor(name, shape, dt))

        def sem(name):
            return ctx.enter_context(nc.semaphore(name))

        xT = [sb(f"xT{n}", [P, 2, IT, B * L], F16) for n in range(3)]
        wT = [sb(f"wT{n}", [P, 2, IT, O3], F16) for n in range(3)]
        woT = sb("woT", [P, 2, IT, D], F16)
        ternT = sb("ternT", [P, IT, D], F16)
        q_pack = [sb(f"q_pack{i}", [P, STEP_COLS], F16) for i in range(NBUF)]
        k_pack = [sb(f"k_pack{i}", [P, STEP_COLS], F16) for i in range(NBUF)]
        v_pack = [sb(f"v_pack{i}", [P, 512]) for i in range(NBUF)]
        probs = sb("probs", [P, PSLOTS, 512])
        sums = sb("sums", [P, 4, 512])
        qk_stage = [sb(f"qk_stage{i}", [P, 2, QK_TILES, BLK], F16) for i in range(2)]
        v_stage = [sb(f"v_stage{i}", [P, 2, D]) for i in range(2)]
        row_max = sb("row_max", [P, 2, 16])
        shift = [sb(f"shift{h}", [16, 128], F16) for h in range(2)]
        shift_hi = sb("shift_hi", [16, 128], F16)
        shift_scale = sb("shift_scale", [16, 2])
        shift_big = sb("shift_big", [16, 128])
        recips = sb("recips", [P, 128])
        attn = sb("attn", [P, 512])
        attn_n = sb("attn_n", [P, 512])
        ident = sb("ident", [P, P])
        ones = sb("ones", [P, P])
        sum_sel = sb("sum_sel", [P, 4, DH])
        spread_sel = sb("spread_sel", [P, 4, P])
        bias_col = sb("bias_col", [P, 3, QK_TILES])
        bias_v = sb("bias_v", [P, 3, D])
        sc = sb("sc", [P, 3, 16])
        fin = sb("fin", [P, 8])
        row_add = sb("row_add", [P, D])
        alpha = sb("alpha", [P, 1])
        stats = sb("stats", [P, 16, 6])
        mv = sb("mv", [P, 16, 2])
        rs = sb("rs", [P, 6, 16])
        prep2 = xT[2][:, :, :, :].rearrange("p a b c -> p (a b c)").bitcast(F32)
        prep1 = xT[1][:, :, :, :].rearrange("p a b c -> p (a b c)").bitcast(F32)
        win_n = [prep2[:, n * 1536:(n + 1) * 1536].rearrange("p (a d) -> p a d", a=6) for n in range(3)]
        wout_n = [prep2[:, 4608 + n * 512:4608 + (n + 1) * 512].rearrange("p (a d) -> p a d", a=2) for n in range(3)]
        w_eff = prep2[:, 6144:7680].rearrange("p (a o) -> p a o", a=2)
        tern_n = prep2[:, 7680:8192].rearrange("p (a d) -> p a d", a=2)
        win_t = [prep1[:, n * 1536:(n + 1) * 1536].rearrange("p (a o) -> p a o", a=2) for n in range(3)]
        w_sq = prep1[:, 4608:6144].rearrange("p (a o) -> p a o", a=2)
        b_row = prep1[:, 6144:6912]
        b_sq = prep1[:, 6912:7680]
        bout_bc = prep1[:, 7680:7936].rearrange("p (a m) -> p a m", a=2)
        bin_row = [q_pack[n][:, :].bitcast(F32)[:, 0:O3] for n in range(3)]
        bin_col = sb("bin_col", [P, 3, QK_TILES])
        bout_col = sb("bout_col", [P, 3, IT])
        bout2_row = v_stage[0][:, 0, :]
        x_ln = probs[:, :, :].rearrange("p a (t d) -> p (a t) d", d=D)
        x_fin = [qk_stage[i // 2][:, i % 2, :, :].rearrange("p o r -> p (o r)").bitcast(F32)[:, 0:D] for i in range(4)]
        y_fin = [probs[:, i, D:2 * D] for i in range(4)]
        o_fin = [probs[:, 4 + i, 0:D] for i in range(4)]

        ps = ctx.enter_context(nc.psum_tensor("ps", [P, 8, 512], F32))
        T_BANK, T_BANKS, O_BANK, D_BANK = 2, 4, 6, 7
        QK_BANK, V_BANK = 2, 6

        win_in = [sem(f"win_in{n}") for n in range(3)]
        small_in = sem("small_in")
        consts_ready = sem("consts_ready")
        pool_chain = sem("pool_chain")
        dve_chain = sem("dve_chain")
        wt_turned = sem("wt_turned")
        wt_copied = sem("wt_copied")
        bout_spread = sem("bout_spread")
        fused = sem("fused")
        fused_copied = sem("fused_copied")
        biased = sem("biased")
        squared = sem("squared")
        sq_summed = sem("sq_summed")
        roots_wanted = sem("roots_wanted")
        roots = sem("roots")
        w_split = sem("w_split")
        last_ready = sem("last_ready")
        last_summed = sem("last_summed")
        last_turned = sem("last_turned")
        x_in = sem("x_in")
        ln_var = sem("ln_var")
        ln_root = sem("ln_root")
        ln_scale = sem("ln_scale")
        ln_applied = sem("ln_applied")
        ln_turned = sem("ln_turned")
        ln_hi = sem("ln_hi")
        ln_lo = sem("ln_lo")
        lin_done = sem("lin_done")
        qk_hi = sem("qk_hi")
        qk_lo = sem("qk_lo")
        v_out = sem("v_out")
        qk_stored = [sem(f"qk_stored{i}") for i in range(2)]
        v_stored = [sem(f"v_stored{i}") for i in range(2)]
        packed = [sem(f"packed{i}") for i in range(NBUF)]
        scored = sem("scored")
        maxed = sem("maxed")
        doubled = sem("doubled")
        turned = sem("turned")
        split_hi = sem("split_hi")
        shift_in = [sem(f"shift_in{h}") for h in range(2)]
        scored_t = sem("scored_t")
        exped = sem("exped")
        bursts = sem("bursts")
        summed = sem("summed")
        ones_done = sem("ones_done")
        recip_done = sem("recip_done")
        o_copied = sem("o_copied")
        spread = sem("spread")
        normed = sem("normed")
        x_hi = sem("x_hi")
        x_lo = sem("x_lo")
        xf_in = [sem(f"xf_in{i}") for i in range(4)]
        row_added = sem("row_added")
        fin_mm = sem("fin_mm")
        fin_y = sem("fin_y")
        fin_acc = sem("fin_acc")
        fin_o = sem("fin_o")
        stored = [sem(f"stored{i}") for i in range(4)]

        block = ctx.enter_context(nc.Block())

        steps = [lv.steps for lv in LEVELS]
        lin_blocks = [r // BLK for r in rows_of]
        GX, U2, SV, RT, RV, GW, SX, GQ, GXN, ESC, TMP, TMP2 = range(12)
        SMALL_DMAS = 13
        QK_STORES = 4 * 16

        g_base = [sum(steps[:n]) for n in range(4)]
        b_base = [sum(lin_blocks[:n]) for n in range(4)]
        u_base = [sum(m.units * m.steps for m in LEVELS[:n]) for n in range(4)]
        v_base = [sum(m.bursts * m.steps for m in LEVELS[:n]) for n in range(4)]
        d_base = [sum(m.sum_bursts * m.steps for m in LEVELS[:n]) for n in range(4)]
        r_base = [sum((m.units + 2) * m.steps for m in LEVELS[:n]) for n in range(4)]

        def packed_base(n, i):
            return sum(16 * per_step_dmas(m) * len(range(i, LEVELS[m].steps, NBUF)) for m in range(n))

        def per_step_dmas(n):
            return 5 if n == 0 else 3

        def first_block(n):
            items = [("L", g) for g in range(QK_TILES + 1)]
            if n:
                tail = LEVELS[n - 1].tokens(False, False, True)
                items[4:4] = tail[4:]
                items[2:2] = tail[2:4]
                items[1:1] = tail[:2]
            return items

        def middle_blocks(n, emit, eng):
            first, last = 2, lin_blocks[n] - 2
            if n == 0:
                for blk in range(first, last):
                    emit(blk, blk % 2)
                return
            with eng.Fori(0, (last - first) // 2) as i:
                for k in range(2):
                    emit(i * 2 + (first + k), k)
            if (last - first) % 2:
                emit(last - 1, (last - 1) % 2)

        def last_blocks(n):
            tokens = LEVELS[n].tokens(False, True, False)
            items, done = [], 0
            for g in range(2 * (QK_TILES + 1)):
                items.append(("L", g))
                upto = min(len(tokens), -(-len(tokens) * g // 8))
                items += tokens[done:upto]
                done = upto
            return items

        def slots(n, emit, eng):
            turns = (steps[n] - NBUF) // NBUF
            emit(0, 0)
            with eng.Fori(0, turns) as i:
                for u in range(NBUF):
                    emit(i * NBUF + (1 + u), (1 + u) % NBUF)
            for s in range(1 + NBUF * turns, steps[n]):
                emit(s, s % NBUF)

        def stores_before(n, k):
            return sum(len(range(k, lin_blocks[m], 2)) for m in range(n))

        def level(n, eng, block, tokens, middle=None, last=None):
            for what, j in first_block(n):
                if what == "L":
                    block(n, 0, 0, j)
                else:
                    tokens(n - 1, steps[n - 1], steps[n - 1] % NBUF, [(what, j)])

            def whole(blk, k):
                for g in range(QK_TILES + 1):
                    block(n, blk, k, g)

            whole(1, 1)
            if middle:
                middle(n)
            middle_blocks(n, whole, eng)
            if last:
                last(n)
            for what, j in last_blocks(n):
                if what == "L":
                    blk = lin_blocks[n] - 2 + j // (QK_TILES + 1)
                    block(n, blk, blk % 2, j % (QK_TILES + 1))
                else:
                    tokens(n, -1, 3, [(what, j)])
            slots(n, lambda s, u: tokens(n, s, u, LEVELS[n].tokens(*parts(n, s))), eng)

        def parts(n, s):
            if not isinstance(s, int):
                return True, True, True
            return 0 <= s < steps[n], s + 1 < steps[n], s >= 1

        def src_row(lv, s, u):
            if lv.n == 0:
                return s * lv.stride
            if lv.n == 1:
                return (s - u % 2) * (lv.stride // 2) + (u % 2) * lv.in_rows
            return (s - u % 4) * (lv.stride // 4) + (u % 4 // 2) * lv.in_rows

        def dst_row(lv, s, u):
            if lv.n == 0:
                return s * lv.T
            if lv.n == 1:
                return (s - u % 2) * (lv.T // 2) + (u % 2) * L
            return (s - u % 4) * (lv.T // 4) + (u % 4 // 2) * L

        OUT_ROWS0 = LEVELS[1].in_rows

        def prob_slot(lv, u, unit):
            return (4 * (u % 2) + unit) if lv.n == 0 else unit % PSLOTS

        def out_slices(lv, s, u, hl):
            x = xT[(lv.n + 1) % 3] if lv.n < 2 else xT[1]
            r = dst_row(lv, s, u)
            if lv.n == 2:
                return [x[:, hl, u % 2, ds(r, 512)]], [attn_n[:, :]]
            if lv.n == 1:
                return [x[:, hl, :, ds(r, 256)]], [attn_n[:, :].rearrange("p (g q) -> p g q", g=2)]
            return ([x[:, hl, :, ds(r + b * OUT_ROWS0, 128)] for b in range(B)],
                    [attn_n[:, b * 256:(b + 1) * 256].rearrange("p (g q) -> p g q", g=2) for b in range(B)])

        @block.gpsimd
        def _(pool):
            n = 0

            def link(ins):
                nonlocal n
                n += 1
                ins.then_inc(pool_chain, 1)
                pool.wait_ge(pool_chain, n)

            link(pool.memset(ident[:, :], 0.0))
            link(pool.affine_select(out=ident[:, :], in_=ident[:, :], compare_op=ALU.not_equal, fill=1.0,
                                    base=0, pattern=[[-1, P]], channel_multiplier=1))
            link(pool.memset(ones[:, :], 1.0))
            link(pool.memset(sum_sel[:, :, :], 0.0))
            sel = sum_sel[:, :, :].rearrange("p a (b c) -> p a b c", b=4)
            link(pool.affine_select(out=sel, in_=sel, compare_op=ALU.not_equal, fill=1.0,
                                    base=0, pattern=[[1, 4], [-1, 4], [0, 8]], channel_multiplier=0))
            link(pool.memset(spread_sel[:, :, :], 0.0))
            sel = spread_sel[:, :, :].rearrange("p a (b c) -> p a b c", b=4)
            link(pool.affine_select(out=sel, in_=sel, compare_op=ALU.not_equal, fill=1.0,
                                    base=0, pattern=[[-8, 4], [-32, 4], [0, 32]], channel_multiplier=1))
            for i in range(NBUF):
                two = k_pack[i][SHIFT_ROW:SHIFT_ROW + 2, :]
                link(pool.memset(two, SHIFT_HI))
                link(pool.affine_select(out=two, in_=two, compare_op=ALU.not_equal, fill=SHIFT_LO,
                                        base=-1, pattern=[[0, STEP_COLS]], channel_multiplier=1))
            link(pool.memset(shift_scale[:, 0:1], -1.0 / SHIFT_LO))
            link(pool.memset(shift_scale[:, 1:2], SHIFT_HI / SHIFT_LO))
            link(pool.memset(shift_scale[0:8, 0:1], -1.0 / SHIFT_HI))
            link(pool.memset(shift_scale[0:8, 1:2], 0.0))
            pool.sem_inc(consts_ready, 1)

            pool.sem_inc(x_lo, 1)
            pool.sem_inc(summed, 8)

            def low_half(lv, s, u):
                pool.wait_ge(x_hi, s + (g_base[lv.n] + 1))
                dst, src = out_slices(lv, s, u, 1)
                hi, _ = out_slices(lv, s, u, 0)
                for k, (d, h, a) in enumerate(zip(dst, hi, src)):
                    ins = pool.tensor_tensor(d, a, h, ALU.subtract)
                ins.then_inc(x_lo, 1)

            for lv in LEVELS:
                def emit(s, u, lv=lv, u0=u_base[lv.n], d0=d_base[lv.n]):
                    has_c, _, has_n = parts(lv.n, s)
                    for k, (unit, a, b, o) in enumerate(lv.sum_jobs()):
                        if has_n and lv.n == 2 and k == 4:
                            low_half(lv, s - 1, (u - 1) % NBUF)
                        if not has_c:
                            continue
                        if k % 4 == 0:
                            pool.wait_ge(ones_done, s * 2 + (d0 + 8 + k // 4 - (lv.n == 1)))
                        pool.wait_ge(exped, s * lv.units + (u0 + T_BANKS + unit + 1))
                        pool.tensor_tensor(sums[:, o[0], o[1]:o[1] + o[2]], probs[:, a[0] % PSLOTS, a[1]:a[1] + a[2]],
                                           probs[:, b[0] % PSLOTS, b[1]:b[1] + b[2]], ALU.add).then_inc(summed, 1)
                    if has_n and lv.n < 2:
                        low_half(lv, s - 1, (u - 1) % NBUF)
                slots(lv.n, emit, pool)
                emit(lv.steps, lv.steps % NBUF)

            pool.wait_ge(row_added, 1)
            pool.wait_ge(bursts, PSLOTS + v_base[3])
            with pool.Fori(0, B * L // P // 4) as i:
                for j in range(4):
                    pool.wait_ge(xf_in[j], i * 16 + 16)
                    pool.wait_ge(fin_o, i * 4 + (j + 1))
                    pool.tensor_tensor(y_fin[j], x_fin[j], row_add[:, :], ALU.add).then_inc(fin_y, 1)

        @block.sync
        def _(sp):
            for k in range(2):
                sp.sem_inc(qk_stored[k], QK_STORES)
                sp.sem_inc(v_stored[k], 16)
            for j in range(4):
                sp.sem_inc(stored[j], 16)
            for n in range(3):
                sp.dma_start(win_n[n], t[f"L0_attn_Win{n}"].rearrange("(a p) d -> p a d", p=P)).then_inc(win_in[n], 16)
                sp.dma_start(wout_n[n], t[f"L0_attn_Wout{n}"].rearrange("(a p) d -> p a d", p=P)).then_inc(win_in[n], 16)
            with nc.allow_non_contiguous_dma(reason="short bias columns"):
                for n in range(3):
                    sp.dma_start(bin_col[:, n, :], t[f"L0_attn_bin{n}"][0:QK_TILES * P].rearrange("(a p) -> p a", p=P)).then_inc(small_in, 16)
                    sp.dma_start(bout_col[:, n, :], t[f"L0_attn_bout{n}"].rearrange("(a p) -> p a", p=P)).then_inc(small_in, 16)
            sp.dma_start(bout2_row, t["L0_attn_bout2"].rearrange("(o n) -> o n", o=1).broadcast_to((P, D))).then_inc(small_in, 16)
            sp.dma_start(row_add[:, :], t["L0_ffn_bias"].rearrange("(o n) -> o n", o=1).broadcast_to((P, D))).then_inc(small_in, 16)
            sp.dma_start(alpha[:, :], t["L0_ffn_alpha"].rearrange("(o n) -> o n", o=1).broadcast_to((P, 1))).then_inc(small_in, 16)
            sp.dma_start(tern_n, t["L0_ffn_weight"].rearrange("(a p) d -> p a d", p=P)).then_inc(small_in, 16)
            for n in range(3):
                sp.dma_start(bin_row[n], t[f"L0_attn_bin{n}"].rearrange("(o n) -> o n", o=1).broadcast_to((P, O3))).then_inc(small_in, 16)
            for b in range(B):
                if b:
                    sp.wait_ge(ln_turned, 8)
                sp.dma_start(x_ln, x_d[b * L:(b + 1) * L, :].rearrange("(a p) d -> p a d", p=P)).then_inc(x_in, 16)

            def all_stored(n, blocks):
                for k in range(2):
                    count = stores_before(n, k) + len(range(k, blocks, 2)) + 1
                    sp.wait_ge(qk_stored[k], QK_STORES * count)
                    sp.wait_ge(v_stored[k], 16 * count)

            def block(n, blk, k, group):
                if group < QK_TILES:
                    return
                sp.wait_ge(qk_lo, blk * QK_TILES + (QK_TILES * (b_base[n] + 1) + QK_TILES))
                dst = qk_d[n].rearrange("o p s r -> p o s r")
                for strip, half, o0, o1 in ((1, 0, 0, 4), (2, 1, 0, 4), (0, 0, 0, 2), (0, 1, 2, 4)):
                    sp.dma_start(dst[:, o0:o1, strip, ds(blk * BLK, BLK)], qk_stage[k][:, half, o0:o1, :]).then_inc(qk_stored[k], 16)
                sp.wait_ge(v_out, blk + (b_base[n] + 2))
                sp.dma_start(v_d[n].rearrange("(n a p) d -> n p a d", p=P, a=2)[ds(blk, 1), :, :, :].rearrange("n p a d -> (n p) a d"),
                             v_stage[k][:, :, :]).then_inc(v_stored[k], 16)

            def load(n, s, u):
                lv, i = LEVELS[n], u % NBUF
                past = s - (NBUF - 1)
                if isinstance(s, int):
                    past = max(past, 0)
                sp.wait_ge(bursts, past * lv.bursts + (v_base[n] + PSLOTS))
                r = src_row(lv, s, u)
                o0, on = (0, 2) if n < 2 else (u % 2, 1)
                for b in range(lv.batches):
                    row = r + b * lv.in_rows
                    c0, c1 = b * lv.heads * lv.T, (b + 1) * lv.heads * lv.T
                    for pack, tile0 in ((q_pack[i], 0), (k_pack[i], IT)):
                        src = qk_d[n][tile0 + o0:tile0 + o0 + on, :, :, ds(row, lv.T)]
                        sp.dma_start(pack[0:SHIFT_ROW, c0:c1].rearrange("p (h r) -> p h r", r=lv.T),
                                     src.rearrange("o (h p) s r -> (p s) (o h) r", p=DH)).then_inc(packed[i], 16)
                if n == 0:
                    src = v_d[n].rearrange("(b r) d -> r b d", b=B)[ds(r, P), :, :]
                elif n == 1:
                    src = v_d[n][ds(r, lv.T), :].rearrange("(a p) d -> p a d", p=P)
                else:
                    src = v_d[n][ds(r, lv.T), (u % 2) * P:(u % 2 + 1) * P].rearrange("(a p) d -> p a d", p=P)
                dst = v_pack[i][:, :].rearrange("p (a d) -> p a d", a=4 if n == 2 else 2)
                sp.dma_start(dst, src).then_inc(packed[i], 16)

            def tokens(n, s, u, todo):
                lv = LEVELS[n]
                if len(todo) > 1 and (not isinstance(s, int) or s + 3 < lv.steps):
                    if isinstance(s, int) and s == 0:
                        all_stored(n, lin_blocks[n])
                        if n == 2:
                            for j in range(4):
                                sp.dma_start(x_fin[j], x_d[j * P:(j + 1) * P, :]).then_inc(xf_in[j], 16)
                    load(n, s + 3, (u + 3) % NBUF)
                for what, h in todo:
                    if what == "M":
                        sp.wait_ge(maxed, s * (lv.units + 2) + (r_base[n] + lv.units + 2 + lv.ring("M", h) + 3))
                        sp.dma_start(q_pack[(u + 1) % NBUF][SHIFT_ROW:SHIFT_ROW + 2, h * 1024:(h + 1) * 1024],
                                     shift[h][:, :]).then_inc(shift_in[h], 16)

            def first_loads(n):
                all_stored(n, (LEVELS[n].in_rows + 2 * BLK - 1) // BLK + (n == 2))
                for s in range(NBUF - 1):
                    load(n, s, s)

            for lv in LEVELS:
                level(lv.n, sp, block, tokens, last=first_loads)

            turns = B * L // P // 4
            with sp.Fori(0, turns - 1) as i:
                for j in range(4):
                    sp.wait_ge(fin_y, i * 4 + (j + 1))
                    sp.dma_start(x_fin[j], x_d[ds(i * (4 * P) + (4 + j) * P, P), :]).then_inc(xf_in[j], 16)
                    sp.wait_ge(fin_o, i * 4 + (j + 5))
                    sp.dma_start(out_d[ds(i * (4 * P) + j * P, P), :], o_fin[j]).then_inc(stored[j], 16)
            for j in range(4):
                sp.wait_ge(fin_o, 4 * turns + j + 1)
                sp.dma_start(out_d[(4 * turns - 4 + j) * P:(4 * turns - 3 + j) * P, :], o_fin[j]).then_inc(stored[j], 16)
            for j in range(4):
                sp.wait_ge(stored[j], 16 * (turns + 1))

        PRODUCTS = ((0, 0), (1, 0), (0, 1))

        @block.tensor
        def _(pe):
            pe.sem_inc(bursts, PSLOTS)
            pe.sem_inc(ones_done, 8)
            pe.wait_ge(consts_ready, 1)

            for n in range(3):
                pe.wait_ge(win_in[n], 32)
                if n:
                    pe.wait_ge(wt_copied, n)
                for it in range(IT):
                    for o in range(6):
                        m = pe.transpose(ps[:, 2 * it + o // 3, (o % 3) * P:(o % 3 + 1) * P],
                                         win_n[n][:, o, it * P:(it + 1) * P], ident[:, :])
                m.then_inc(wt_turned, 1)
            pe.wait_ge(wt_copied, 3)
            for n in range(3):
                if n:
                    if n > 1:
                        pe.wait_ge(fused_copied, n - 1)
                        pe.wait_ge(biased, n)
                    for it in range(IT):
                        for oh in range(2):
                            for jt in range(IT):
                                pe.matmul(ps[:, 2 * it + oh, 0:384], wout_n[n - 1][:, jt, it * P:(it + 1) * P],
                                          win_t[n][:, jt, oh * 384:(oh + 1) * 384], start=jt == 0, stop=jt == 1)
                    pe.wait_ge(bout_spread, n)
                    for oh in range(2):
                        for jt in range(IT):
                            pe.matmul(ps[:, 4 + oh, 0:384], bout_bc[:, jt, :],
                                      win_t[n][:, jt, oh * 384:(oh + 1) * 384], start=jt == 0, stop=jt == 1)
                    for o in range(QK_TILES):
                        for jt in range(IT):
                            m = pe.matmul(ps[:, 5, 400 + o:401 + o], win_t[n][:, jt, o * P:(o + 1) * P],
                                          bout_col[:, n - 1, jt:jt + 1], start=jt == 0, stop=jt == 1)
                    m.then_inc(fused, 1)
                pe.wait_ge(squared, n + 1)
                for oh in range(2):
                    for jt in range(IT):
                        m = pe.matmul(ps[:, 6 + oh, 0:384], ones[:, :], w_sq[:, jt, oh * 384:(oh + 1) * 384],
                                      start=jt == 0, stop=jt == 1)
                m.then_inc(sq_summed, 1)
            pe.wait_ge(last_ready, 1)
            pe.wait_ge(fused_copied, 2)
            m = pe.matmul(ps[:, 4, 0:2], ones[:, :], fin[:, 0:2], start=True, stop=True)
            m.then_inc(last_summed, 1)
            for it in range(IT):
                for a in range(2):
                    pe.transpose(ps[:, 0, it * D + a * P:it * D + (a + 1) * P],
                                 wout_n[2][:, a, it * P:(it + 1) * P], ident[:, :])
            pe.wait_ge(last_ready, 2)
            for it in range(IT):
                for a in range(2):
                    m = pe.transpose(ps[:, 1, it * D + a * P:it * D + (a + 1) * P],
                                     tern_n[:, a, it * P:(it + 1) * P], ident[:, :])
            m.then_inc(last_turned, 1)
            pe.wait_ge(w_split, 4)

            for b in range(B):
                for q in range(8):
                    g = 8 * b + q
                    pe.wait_ge(ln_applied, 16 * b + 2 * q + 2)
                    pe.wait_ge(ln_lo, g + 1)
                    for a in range(2):
                        for it in range(IT):
                            m = pe.transpose(ps[:, g % 4, it * 256 + a * P:it * 256 + (a + 1) * P],
                                             x_ln[:, 2 * q + a, it * P:(it + 1) * P], ident[:, :])
                    m.then_inc(ln_turned, 1)
            pe.wait_ge(ln_lo, 16 + 4)

            def block(n, blk, k, group):
                x, w, b0 = xT[n], wT[n], b_base[n]
                first = isinstance(blk, int) and blk == 0
                if n == 0:
                    b, j = divmod(blk, lin_blocks[0] // B)
                    col = b * L + j * BLK
                else:
                    col = blk * BLK
                if group < QK_TILES:
                    o = group
                    if first and group == 0 and n:
                        pe.wait_ge(x_lo, g_base[n] - 1)
                        pe.wait_ge(exped, u_base[n] + T_BANKS)
                    pe.wait_ge(qk_lo, blk * QK_TILES + (QK_TILES * b0 + o + 1))
                    for it in range(IT):
                        for i, (wh, xh) in enumerate(PRODUCTS):
                            m = pe.matmul(ps[:, QK_BANK + o, 0:BLK], w[:, wh, it, o * P:(o + 1) * P], x[:, xh, it, ds(col, BLK)],
                                          start=it + i == 0, stop=it == 1 and i == 2)
                else:
                    if first:
                        pe.wait_ge(normed, g_base[n] + 1)
                    pe.wait_ge(v_out, blk + (b0 + 1))
                    for a in range(2):
                        for it in range(IT):
                            for i, (wh, xh) in enumerate(PRODUCTS):
                                m = pe.matmul(ps[:, V_BANK, a * D:(a + 1) * D], x[:, xh, it, ds(col + a * P, P)],
                                              w[:, wh, it, 2 * D:3 * D],
                                              start=it + i == 0, stop=it == 1 and i == 2)
                m.then_inc(lin_done, 1)

            def input_complete(n):
                if n:
                    pe.wait_ge(x_lo, g_base[n] + 1)

            def tokens(n, s, u, todo):
                    lv, g0, u0, v0, r0 = LEVELS[n], g_base[n], u_base[n], v_base[n], r_base[n]
                    at_start = isinstance(s, int) and s == 0
                    qc, kc, vc = q_pack[u], k_pack[u], v_pack[u]
                    qb, kb = q_pack[(u + 1) % NBUF], k_pack[(u + 1) % NBUF]
                    ring0 = r0 + lv.units + 2
                    for what, j in todo:
                        of, v_of, t_of = (s - 1, v_pack[u - 1], u - 1) if what in "WE" else (s, vc, u)
                        j = {"W": lv.bursts - 1, "E": lv.sum_bursts - 1}.get(what, j)
                        if what == "S":
                            bank = lv.ring("S", j)
                            if j == 0:
                                nb = (u + 1) % NBUF
                                pe.wait_ge(packed[nb], (s + 1 - nb) * (4 * per_step_dmas(n)) + (packed_base(n, nb) + 16 * per_step_dmas(n)))
                            pe.wait_ge(maxed, s * (lv.units + 2) + (ring0 + bank + 1))
                            for c, q, k, w_ in lv.query_unit(j):
                                m = pe.matmul(ps[:, bank % 2, c:c + w_], qb[0:SHIFT_ROW, q:q + P], kb[0:SHIFT_ROW, k:k + w_],
                                              start=True, stop=True)
                            m.then_inc(scored, 1)
                        elif what == "M":
                            bank = lv.ring("M", j)
                            pe.wait_ge(maxed, s * (lv.units + 2) + (ring0 + bank + 1))
                            pe.wait_ge(doubled, s * 2 + (2 * g0 + 2 + j + 1))
                            pe.transpose(ps[0:16, bank % 2, 0:P], row_max[:, j, :], ident[:, :]).then_inc(turned, 1)
                        elif what == "T":
                            if j == 0 or lv.shift_half(j) != lv.shift_half(j - 1):
                                pe.wait_ge(shift_in[lv.shift_half(j)], s * 16 + (16 * g0 + 16))
                            if j == 0 and at_start:
                                pe.wait_ge(qk_lo, QK_TILES * (b_base[n + 1] + 1))
                            pe.wait_ge(exped, s * lv.units + (u0 + j + 1))
                            for c, k, q, w_ in lv.key_unit(j):
                                m = pe.matmul(ps[:, T_BANK + j % T_BANKS, c:c + w_], kc[0:SHIFT_ROW + 2, k:k + P],
                                              qc[0:SHIFT_ROW + 2, q:q + w_], start=True, stop=True)
                            m.then_inc(scored_t, 1)
                        elif what in "VW":
                            pe.wait_ge(exped, of * lv.units + (u0 + (j + 1) * lv.per_burst + T_BANKS))
                            if j == 0 and at_start:
                                pe.wait_ge(v_out, b_base[n + 1] + 1)
                            if j == 0:
                                pe.wait_ge(normed, s + (g0 + 1))
                            for quad, unit, c, w_, vcol, oc, first, last in lv.value_products(j):
                                p = probs[:, prob_slot(lv, t_of, unit), c:c + w_]
                                m = pe.matmul(ps[quad * DH:(quad + 1) * DH, O_BANK, oc:oc + w_], v_of[:, vcol:vcol + DH], p,
                                              start=first, stop=last)
                            m.then_inc(bursts, 1)
                        elif what in "DE":
                            if lv.sums:
                                pe.wait_ge(summed, of * lv.sums + (lv.sums * (g0 - steps[0]) + 8 + 4 * (j + 1)))
                            if j == 0:
                                pe.wait_ge(recip_done, s + (g0 + 1))
                            for quad, buf, c, slab, first, last in lv.sum_products(j):
                                p = (sums[:, buf, c:c + P] if lv.sums else probs[:, prob_slot(lv, t_of, buf), c:c + P])
                                m = pe.matmul(ps[quad * DH:(quad + 1) * DH, D_BANK, 0:P], sum_sel[:, slab, :], p,
                                              start=first, stop=last)
                            m.then_inc(ones_done, 1)
                        elif what == "N":
                            pe.wait_ge(recip_done, s + (g0 + 1))
                            pe.wait_ge(o_copied, s + g0)
                            for j4 in range(4):
                                m = pe.matmul(ps[:, O_BANK, j4 * P:(j4 + 1) * P], spread_sel[:, j4, :], recips[:, :],
                                              start=True, stop=True)
                            m.then_inc(spread, 1)
            for lv in LEVELS:
                level(lv.n, pe, block, tokens, middle=input_complete)
            tokens(2, steps[2], 0, LEVELS[2].tokens(False, False, True))

            for b in range(B):
              pe.wait_ge(x_lo, g_base[3] + 1 - (2 if b == 0 else 0))
              with pe.Fori(b * (L // P // 4), (b + 1) * (L // P // 4)) as i:
                for j in range(4):
                    col = i * (4 * P) + j * P
                    pe.wait_ge(fin_o, i * 4 + (j + 1))
                    for it in range(IT):
                        for k, (wh, xh) in enumerate(PRODUCTS):
                            pe.matmul(ps[:, j, 0:D], xT[1][:, xh, it, ds(col, P)], woT[:, wh, it, :],
                                      start=it + k == 0, stop=it == 1 and k == 2)
                    for it in range(IT):
                        for hl in range(2):
                            m = pe.matmul(ps[:, j, D:2 * D], xT[0][:, hl, it, ds(col, P)], ternT[:, it, :],
                                          start=it + hl == 0, stop=it + hl == 2)
                    m.then_inc(fin_mm, 1)

        @block.scalar
        def _(act):
            act.sem_inc(exped, T_BANKS)
            for n in range(3):
                act.wait_ge(wt_turned, n + 1)
                for it in range(IT):
                    for oh in range(2):
                        m = act.activation(win_t[n][:, it, oh * 384:(oh + 1) * 384], ps[:, 2 * it + oh, 0:384], ACT.Copy)
                m.then_inc(wt_copied, 1)
            for n in range(3):
                if n:
                    act.wait_ge(fused, n)
                    if n > 1:
                        act.wait_ge(w_split, n)
                    for it in range(IT):
                        for oh in range(2):
                            m = act.activation(w_eff[:, it, oh * 384:(oh + 1) * 384], ps[:, 2 * it + oh, 0:384], ACT.Copy)
                    m.then_inc(fused_copied, 1)
                act.wait_ge(roots_wanted, n + 1)
                act.activation(sc[:, n, RT:RT + 2], sc[:, n, U2:U2 + 2], ACT.Sqrt).then_inc(roots, 1)
            act.wait_ge(roots_wanted, 4)
            act.activation(fin[:, 3:4], fin[:, 2:3], ACT.Sqrt).then_inc(roots, 1)

            for b in range(B):
                act.wait_ge(ln_var, b + 1)
                act.activation(rs[:, 1, :], rs[:, 0, :], ACT.Sqrt).then_inc(ln_root, 1)
                act.wait_ge(ln_scale, b + 1)
                for q in range(9):
                    if q < 8:
                        for a in range(2):
                            k = 2 * q + a
                            act.activation(x_ln[:, k, :], x_ln[:, k, :], ACT.Identity, scale=rs[:, 4, k:k + 1],
                                           bias=rs[:, 5, k:k + 1]).then_inc(ln_applied, 1)
                    if q:
                        g = 8 * b + q - 1
                        act.wait_ge(ln_turned, g + 1)
                        act.activation(xT[0][:, 0, :, g * 256:(g + 1) * 256],
                                       ps[:, g % 4, :].rearrange("p (a r) -> p a r", a=IT), ACT.Copy).then_inc(ln_hi, 1)

            def block(n, blk, k, group):
                if group == QK_TILES:
                    return
                if group == 0:
                    act.wait_ge(qk_stored[k], (blk - k) * (QK_STORES // 2) + QK_STORES * (stores_before(n, k) + 1))
                act.wait_ge(lin_done, blk * (QK_TILES + 1) + ((QK_TILES + 1) * b_base[n] + group + 1))
                act.activation(qk_stage[k][:, group // IT, group, :], ps[:, QK_BANK + group, 0:BLK], ACT.Identity,
                               bias=bias_col[:, n, group:group + 1]).then_inc(qk_hi, 1)

            def tokens(n, s, u, todo):
                    lv, g0, u0, v0 = LEVELS[n], g_base[n], u_base[n], v_base[n]
                    for what, j in todo:
                        if what == "T":
                            act.wait_ge(scored_t, s * lv.units + (u0 + j + 1))
                            if n == 0:
                                act.wait_ge(ones_done, s * lv.units + (j + 1))
                            else:
                                act.wait_ge(bursts, s * lv.bursts + (PSLOTS + v0 + j // 4 - 1))
                                k = j if n == 1 else 4 * (j // 8 + 1) + j % 4
                                act.wait_ge(summed, s * lv.sums + (lv.sums * (g0 - steps[0]) + k + 1))
                            act.activation(probs[:, prob_slot(lv, u, j), :], ps[:, T_BANK + j % T_BANKS, :], ACT.Exp,
                                           scale=sc[:, n, ESC:ESC + 1]).then_inc(exped, 1)
                        elif what == "O":
                            act.wait_ge(bursts, s * lv.bursts + (PSLOTS + v0))
                            act.wait_ge(normed, s + g0)
                            act.activation(attn[:, :], ps[:, O_BANK, :], ACT.Copy).then_inc(o_copied, 1)
                        elif what == "H":
                            act.wait_ge(normed, s + (g0 + 1))
                            dst, src = out_slices(lv, s - 1, (u - 1) % NBUF, 0)
                            for d, a in zip(dst, src):
                                m = act.activation(d, a, ACT.Copy)
                            m.then_inc(x_hi, 1)
            for lv in LEVELS:
                level(lv.n, act, block, tokens)
            tokens(2, steps[2], 0, LEVELS[2].tokens(False, False, True))

        @block.vector
        def _(dve):
            chained = 0

            def link(ins):
                nonlocal chained
                chained += 1
                ins.then_inc(dve_chain, 1)
                dve.wait_ge(dve_chain, chained)

            def power_of_two(to, of, bound):
                link(dve.reciprocal(to, of))
                link(dve.tensor_scalar(to, to, bound, None, ALU.mult))
                link(dve.tensor_scalar(to.bitcast(I32), to.bitcast(I32), EXPONENT, None, ALU.bitwise_and))

            dve.sem_inc(maxed, 2)
            dve.sem_inc(recip_done, 1)
            dve.sem_inc(normed, 1)
            dve.sem_inc(qk_lo, QK_TILES)
            dve.sem_inc(v_out, 1)
            dve.sem_inc(ln_lo, 4)
            dve.sem_inc(fin_o, 4)
            dve.wait_ge(consts_ready, 1)
            dve.wait_ge(small_in, 16 * SMALL_DMAS)

            for n in range(3):
                def col(k, w=1, n=n):
                    return sc[:, n, k:k + w]
                if n == 0:
                    w, brow, bcol = win_t[0], bin_row[0], bin_col[:, 0, :]
                    link(dve.memset(col(GX), 1.0))
                    dve.wait_ge(wt_copied, 1)
                else:
                    w, brow, bcol = w_eff, b_row, bin_col[:, n, :]
                    for jt in range(IT):
                        m = dve.tensor_scalar(bout_bc[:, jt, :], ones[:, :], bout_col[:, n - 1, jt:jt + 1], None, ALU.mult)
                    m.then_inc(bout_spread, 1)
                    link(dve.tensor_copy(col(GX), sc[:, n - 1, GXN:GXN + 1]))
                    dve.wait_ge(fused, n)
                    for oh in range(2):
                        dve.tensor_tensor(b_row[:, oh * 384:(oh + 1) * 384], ps[:, 4 + oh, 0:384],
                                          bin_row[n][:, oh * 384:(oh + 1) * 384], ALU.add)
                    link(dve.tensor_tensor(bcol, ps[:, 5, 400:400 + QK_TILES], bcol, ALU.add))
                    dve.wait_ge(fused_copied, n)
                for it in range(IT):
                    m = dve.tensor_tensor(w_sq[:, it, :], w[:, it, :], w[:, it, :], ALU.mult)
                m.then_inc(squared, 1)
                dve.sem_inc(biased, 1)
                link(dve.tensor_scalar(b_sq, brow, col(GX), None, ALU.mult))
                link(dve.tensor_tensor(b_sq, b_sq, b_sq, ALU.mult))
                dve.wait_ge(sq_summed, n + 1)
                r2 = (NORM_BOUND if n == 0 else ROW_BOUND) ** 2
                dve.scalar_tensor_tensor(out=b_sq[:, 0:384], in0=ps[:, 6, 0:384], scalar=r2, in1=b_sq[:, 0:384],
                                         op0=ALU.mult, op1=ALU.add)
                link(dve.scalar_tensor_tensor(out=b_sq[:, 384:768], in0=ps[:, 7, 0:384], scalar=r2, in1=b_sq[:, 384:768],
                                              op0=ALU.mult, op1=ALU.add))
                dve.reduce_max(col(U2), b_sq, AX_X)
                link(dve.reduce_sum(col(SV), b_sq[:, 2 * D:3 * D], AX_X))
                m = dve.tensor_scalar(col(U2, 2), col(U2, 2), 2.0, 1e-30, ALU.mult, ALU.add)
                m.then_inc(roots_wanted, 1)
                dve.wait_ge(roots, n + 1)
                power_of_two(col(GW), col(RT), ACC_BOUND)
                link(dve.tensor_tensor(col(TMP), col(RV), col(GW), ALU.mult))
                power_of_two(col(SX), col(TMP), ROW_BOUND)
                link(dve.tensor_tensor(col(GQ), col(GX), col(GW), ALU.mult))
                dve.tensor_tensor(col(GXN), col(GQ), col(SX), ALU.mult)
                link(dve.tensor_tensor(col(TMP), col(GQ), col(GQ), ALU.mult))
                link(dve.reciprocal(col(TMP2), col(TMP)))
                dve.tensor_scalar(col(ESC), col(TMP2), float(DH) ** -0.5, None, ALU.mult)
                dve.tensor_scalar(bias_col[:, n, :], bcol, col(GQ), None, ALU.mult)
                dve.tensor_scalar(bias_v[:, n, :], brow[:, 2 * D:3 * D], col(GXN), None, ALU.mult)
                for it in range(IT):
                    m = dve.tensor_scalar(wT[n][:, 0, it, :], w[:, it, :], col(GW), None, ALU.mult)
                link(m)
                for it in range(IT):
                    m = dve.scalar_tensor_tensor(out=wT[n][:, 1, it, :], in0=w[:, it, :], scalar=col(GW),
                                                 in1=wT[n][:, 0, it, :], op0=ALU.mult, op1=ALU.subtract)
                m.then_inc(w_split, 1)
                dve.wait_ge(w_split, n + 1)
            link(dve.tensor_tensor(w_sq[:, 0, 0:2 * D].rearrange("p (a d) -> p a d", a=2), wout_n[2], wout_n[2], ALU.mult))
            dve.reduce_sum(fin[:, 0:1], w_sq[:, 0, 0:2 * D], AX_X)
            dve.tensor_reduce(fin[:, 1:2], tern_n, mybir.AxisListType.XY, ALU.add, apply_absolute_value=True).then_inc(last_ready, 1)
            link(dve.tensor_tensor(row_add[:, :], row_add[:, :], bout2_row, ALU.add))
            dve.wait_ge(last_summed, 1)
            dve.tensor_scalar(fin[:, 2:3], ps[:, 4, 0:1], 1e-30, None, ALU.add).then_inc(roots_wanted, 1)
            dve.tensor_scalar(fin[:, 4:5], ps[:, 4, 1:2], 1.0 / (D * D), 0.7, ALU.mult, ALU.mult)
            link(dve.tensor_scalar(fin[:, 5:6], ps[:, 4, 1:2], 1.0 / (D * D), -0.7, ALU.mult, ALU.mult))
            sq = w_sq[:, 0, 0:2 * D].rearrange("p (a d) -> p a d", a=2)
            link(dve.tensor_scalar(sq, tern_n, fin[:, 5:6], None, ALU.is_lt))
            link(dve.tensor_scalar(tern_n, tern_n, fin[:, 4:5], None, ALU.is_gt))
            dve.tensor_tensor(tern_n, tern_n, sq, ALU.subtract).then_inc(last_ready, 1)
            dve.wait_ge(roots, 4)
            power_of_two(fin[:, 6:7], fin[:, 3:4], ACC_BOUND)
            link(dve.tensor_tensor(fin[:, 7:8], fin[:, 6:7], sc[:, 2, GXN:GXN + 1], ALU.mult))
            link(dve.reciprocal(fin[:, 7:8], fin[:, 7:8]))
            dve.wait_ge(last_turned, 1)
            wo = ps[:, 0, :].rearrange("p (a d) -> p a d", a=IT)
            link(dve.tensor_scalar(woT[:, 0, :, :], wo, fin[:, 6:7], None, ALU.mult))
            dve.scalar_tensor_tensor(out=woT[:, 1, :, :], in0=wo, scalar=fin[:, 6:7], in1=woT[:, 0, :, :],
                                     op0=ALU.mult, op1=ALU.subtract)
            dve.tensor_copy(ternT[:, :, :], ps[:, 1, :].rearrange("p (a d) -> p a d", a=IT)).then_inc(w_split, 1)
            dve.sem_inc(row_added, 1)

            for b in range(B):
                dve.wait_ge(x_in, 16 * (b + 1))
                for k in range(16):
                    m = dve.bn_stats(stats[:, k, :], x_ln[:, k, :])
                link(m)
                for k in range(16):
                    m = dve.bn_aggr(mv[:, k, :], stats[:, k, :])
                link(m)
                dve.tensor_scalar(rs[:, 0, :], mv[:, :, 1], EPS, None, ALU.add).then_inc(ln_var, 1)
                dve.wait_ge(ln_root, b + 1)
                link(dve.reciprocal(rs[:, 2, :], rs[:, 1, :]))
                link(dve.tensor_tensor(rs[:, 3, :], rs[:, 2, :], rs[:, 2, :], ALU.mult))
                link(dve.tensor_tensor(rs[:, 3, :], rs[:, 3, :], rs[:, 0, :], ALU.mult))
                link(dve.tensor_scalar(rs[:, 3, :], rs[:, 3, :], -0.5, 1.5, ALU.mult, ALU.add))
                link(dve.tensor_tensor(rs[:, 4, :], rs[:, 2, :], rs[:, 3, :], ALU.mult))
                dve.scalar_tensor_tensor(out=rs[:, 5, :], in0=mv[:, :, 0], scalar=-1.0, in1=rs[:, 4, :],
                                         op0=ALU.mult, op1=ALU.mult).then_inc(ln_scale, 1)
                for q in range(8):
                    g = 8 * b + q
                    dve.wait_ge(ln_hi, g + 1)
                    dve.tensor_tensor(xT[0][:, 1, :, g * 256:(g + 1) * 256], ps[:, g % 4, :].rearrange("p (a r) -> p a r", a=IT),
                                      xT[0][:, 0, :, g * 256:(g + 1) * 256], ALU.subtract).then_inc(ln_lo, 1)

            def block(n, blk, k, group):
                if group == 0:
                    dve.wait_ge(qk_stored[k], (blk - k) * (QK_STORES // 2) + QK_STORES * (stores_before(n, k) + 1))
                if group < QK_TILES:
                    dve.wait_ge(qk_hi, blk * QK_TILES + (QK_TILES * b_base[n] + group + 1))
                    dve.scalar_tensor_tensor(out=qk_stage[k][:, 1 - group // IT, group, :], in0=ps[:, QK_BANK + group, 0:BLK],
                                             scalar=bias_col[:, n, group:group + 1], in1=qk_stage[k][:, group // IT, group, :],
                                             op0=ALU.add, op1=ALU.subtract).then_inc(qk_lo, 1)
                    return
                dve.wait_ge(v_stored[k], (blk - k) * 8 + 16 * (stores_before(n, k) + 1))
                dve.wait_ge(lin_done, blk * (QK_TILES + 1) + (QK_TILES + 1) * (b_base[n] + 1))
                for a in range(2):
                    m = dve.scalar_tensor_tensor(out=v_stage[k][:, a, :], in0=ps[:, V_BANK, a * D:(a + 1) * D],
                                                 scalar=sc[:, n, SX:SX + 1], in1=bias_v[:, n, :],
                                                 op0=ALU.mult, op1=ALU.add)
                m.then_inc(v_out, 1)

            def tokens(n, s, u, todo):
                    lv, g0, u0, d0, r0 = LEVELS[n], g_base[n], u_base[n], d_base[n], r_base[n]
                    for what, j in todo:
                        if what == "S":
                            dve.wait_ge(scored, s * lv.units + (u0 + lv.units + j + 1))
                            c = lv.mx_cols
                            h, c0 = j * c // 8, j * c % 8
                            dve.reduce_max(row_max[:, h, c0:c0 + c], ps[:, lv.ring("S", j) % 2, :].rearrange("p (a k) -> p a k", a=c),
                                           AX_X).then_inc(maxed, 1)
                            if c0 + c == 8:
                                dve.wait_ge(maxed, s * (lv.units + 2) + (r0 + lv.units + 2 + lv.last_scored(h) + 2))
                                dve.tensor_copy(row_max[:, h, 8:16], row_max[:, h, 0:8]).then_inc(doubled, 1)
                        elif what == "M":
                            big = ps[0:16, lv.ring("M", j) % 2, 0:P]
                            dve.wait_ge(turned, s * 2 + (2 * g0 + 2 + j + 1))
                            dve.tensor_scalar(shift_hi[:, :], big, -1.0 / SHIFT_HI, None, ALU.mult).then_inc(split_hi, 1)
                            dve.wait_ge(split_hi, s * 4 + (4 * g0 + 4 + 2 * j + 1))
                            dve.tensor_scalar(shift_big[:, :], shift_hi[:, :], shift_scale[:, 1:2], None,
                                              ALU.mult).then_inc(split_hi, 1)
                            dve.wait_ge(split_hi, s * 4 + (4 * g0 + 4 + 2 * j + 2))
                            if not isinstance(s, int) or s >= 0 or n:
                                dve.wait_ge(shift_in[j], s * 16 + (16 * g0 + 16))
                            dve.scalar_tensor_tensor(out=shift[j][:, :], in0=big, scalar=shift_scale[:, 0:1],
                                                     in1=shift_big[:, :], op0=ALU.mult, op1=ALU.subtract).then_inc(maxed, 1)
                        elif what == "R":
                            dve.wait_ge(ones_done, s * lv.sum_bursts + (d0 + 8))
                            dve.reciprocal(recips[:, :], ps[:, D_BANK, 0:P]).then_inc(recip_done, 1)
                        elif what == "N":
                            dve.wait_ge(spread, s + g0)
                            dve.wait_ge(o_copied, s + g0)
                            dve.wait_ge(x_lo, s + g0)
                            dve.tensor_tensor(attn_n[:, :], attn[:, :], ps[:, O_BANK, :], ALU.mult).then_inc(normed, 1)
            for lv in LEVELS:
                level(lv.n, dve, block, tokens)
            tokens(2, steps[2], 0, LEVELS[2].tokens(False, False, True))

            with dve.Fori(0, B * L // P // 4) as i:
                for j in range(4):
                    dve.wait_ge(fin_mm, i * 4 + (j + 1))
                    dve.wait_ge(fin_y, i * 4 + (j + 1))
                    dve.scalar_tensor_tensor(out=y_fin[j], in0=ps[:, j, 0:D], scalar=fin[:, 7:8], in1=y_fin[j],
                                             op0=ALU.mult, op1=ALU.add).then_inc(fin_acc, 1)
                    dve.wait_ge(fin_acc, i * 4 + (j + 1))
                    dve.wait_ge(stored[j], i * 16 + 16)
                    dve.scalar_tensor_tensor(out=o_fin[j], in0=ps[:, j, D:2 * D], scalar=alpha[:, 0:1], in1=y_fin[j],
                                             op0=ALU.mult, op1=ALU.add).then_inc(fin_o, 1)


_INS = (["L0_attn_x"] + [f"L0_attn_{w}{n}" for n in range(3) for w in ("Win", "bin", "Wout", "bout")]
        + ["L0_ffn_weight", "L0_ffn_alpha", "L0_ffn_bias"])


def kernel(**inputs):
    import numpy as _np
    import concourse.bacc as _bacc
    from concourse import mybir as _mybir
    from concourse.bass_utils import run_bass_kernel_spmd as _run

    nc = _bacc.Bacc("TRN2", target_bir_lowering=False, num_devices=1)
    arrays, handles = {}, {}
    for name in _INS:
        a = _np.ascontiguousarray(inputs[name])
        arrays[f"in_{name}"] = a
        handles[name] = nc.dram_tensor(f"in_{name}", a.shape, _mybir.dt.from_np(a.dtype), kind="ExternalInput").ap()
    out = nc.dram_tensor("out", (B, L, D), F32, kind="ExternalOutput").ap()
    build(nc, handles, out)
    r = _run(nc, [arrays], core_ids=[0])
    return r.results[0]["out"]
```

```python
from contextlib import ExitStack

import concourse.bass as bass
from concourse import mybir

ALU = mybir.AluOpType
ACT = mybir.ActivationFunctionType
AX_X = mybir.AxisListType.X
F32 = mybir.dt.float32
F16 = mybir.dt.float16
I32 = mybir.dt.int32
ds = bass.ds

P = 128
B = 2
L = 2048
D = 256
O3 = 3 * D
DH = 32
IT = D // P
OVERLAP = 64
QK_TILES = 2 * D // P
BLK = 256
STEP_COLS = 2048
NBUF = 4
LOAD_AFTER = (0, 1, 1)
PSLOTS = 8
EXPONENT = 0x7F800000
SHIFT_ROW = 96
SHIFT_HI, SHIFT_LO = 2.0 ** 14, 2.0 ** 3
ACC_BOUND = 2.0 ** 12
ROW_BOUND = 2.0 ** 10
NORM_BOUND = 16.0
EPS = 1e-5


class Level:

    def __init__(self, n, chunk, chunks, in_rows, heads, batches):
        self.n, self.T = n, chunk
        self.stride = chunk - OVERLAP
        self.chunks = chunks
        self.in_rows = in_rows
        self.heads, self.batches = heads, batches
        self.steps = chunks * (B // batches) * (8 // heads)
        self.units = STEP_COLS // 128 * chunk // 512
        self.per_burst = {0: 1, 1: 4, 2: 4}[n]
        self.bursts = self.units // self.per_burst
        self.mx_cols = 16 // self.units
        self.sum_bursts = {0: 4, 1: 2, 2: 2}[n]
        self.sums = {0: 0, 1: 8, 2: 8}[n]

    def query_unit(self, u):
        if self.n == 2:
            return [(0, u * 128, (u // 4) * 512, 512)]
        if self.n == 1:
            return [(qt * 256, u * 256 + qt * 128, u * 256, 256) for qt in range(2)]
        return [(j * 128, (4 * u + j) * 128, (4 * u + j) * 128, 128) for j in range(4)]

    def key_unit(self, u):
        if self.n == 2:
            h, kt = u % 4, u // 4
            return [(0, h * 512 + kt * 128, h * 512, 512)]
        if self.n == 1:
            return [(kt * 256, u * 256 + kt * 128, u * 256, 256) for kt in range(2)]
        return [(j * 128, (4 * u + j) * 128, (4 * u + j) * 128, 128) for j in range(4)]

    def shift_half(self, u):
        if self.n == 2:
            return u % 4 // 2
        return 2 * u // self.units

    def value_products(self, g):
        if self.n == 2:
            return [(q, 4 * g + q, 0, 512, g * 128 + q * DH, 0, g == 0, g == 3) for q in range(4)]
        if self.n == 1:
            return [(q, 4 * g + q, kt * 256, 256, kt * 256 + g * 128 + q * DH, g * 256, kt == 0, kt == 1)
                    for kt in range(2) for q in range(4)]
        return [(q, g, q * 128, 128, (g // 2) * 256 + (g % 2) * 128 + q * DH, g * 128, True, True)
                for q in range(4)]

    def ring(self, what, j):
        return [t for t in ORDER[self.n] if t[0] in "SM"].index((what, j))

    def last_scored(self, h):
        return self.ring("S", (h + 1) * self.units // 2 - 1) + 1

    def sum_jobs(self):
        if self.n == 2:
            return [(4 * (2 * m + 1) + q, (8 * m + q, 0, 512), (8 * m + 4 + q, 0, 512), (q, 0, 512))
                    for m in range(2) for q in range(4)]
        if self.n == 1:
            return [(u, (u, 0, 256), (u, 256, 256), (u // 2, 256 * (u % 2), 256)) for u in range(8)]
        return []

    def sum_products(self, g):
        if self.n == 2:
            return [(q, q, j * 128, j, g == 0 and j == 0, g == 1 and j == 3)
                    for j in range(4) for q in range(4)]
        if self.n == 1:
            return [(q, 2 * g + q // 2, 256 * (q % 2) + qb * 128, 2 * g + qb, g + qb == 0, g + qb == 2)
                    for qb in range(2) for q in range(4)]
        return [(q, g, q * 128, g, g == 0, g == 3) for q in range(4)]

    def tokens(self, has_c=True, has_b=True, has_n=True):
        return [t for t in ORDER[self.n] if (t[0] in "TVD" and has_c) or (t[0] in "SM" and has_b)
                or (t[0] in "WERONH" and has_n)]


def order(text):
    return [(w[0], int(w[1:] or 0)) for w in text.split()]


ORDER = {
    2: order("S0 W S1 O S2 T0 T1 S3 S4 E R T2 T3 S5 T4 T5 S6 N T6 S7 S8 H V0 T7 T8 S9 T9 S10 T10 T11 S11 T12 "
             "S12 V1 S13 M0 D0 S14 T13 S15 T14 T15 V2 M1"),
    1: order("S0 W S1 S2 T0 T1 S3 T2 O S4 E R T3 S5 T4 T5 T6 M0 N S6 S7 T7 H V0 D0 M1"),
    0: order("S0 T0 S1 W S2 O T1 E M0 R S3 V0 T2 T3 N V1 M1 H V2 D0 D1 D2"),
}

LEVELS = [Level(0, 128, 13, 1024, 8, 2), Level(1, 256, 8, 1664, 8, 1), Level(2, 512, 4, 2048, 4, 1)]


def build(nc, t, out):
    x_d = t["L0_attn_x"].rearrange("b l d -> (b l) d")
    out_d = out.rearrange("b l d -> (b l) d")
    rows_of = [B * lv.in_rows for lv in LEVELS]
    qk_d = [nc.dram_tensor(f"qk_scratch{n}", (QK_TILES, P, 3, r), F16, kind="Internal").ap()
            for n, r in enumerate(rows_of)]
    v_d = [nc.dram_tensor(f"v_scratch{n}", (r, D), F32, kind="Internal").ap() for n, r in enumerate(rows_of)]

    ctx = ExitStack()
    with ctx:
        def sb(name, shape, dt=F32):
            return ctx.enter_context(nc.sbuf_tensor(name, shape, dt))

        def sem(name):
            return ctx.enter_context(nc.semaphore(name))

        xT = [sb(f"xT{n}", [P, 2, IT, B * L], F16) for n in range(3)]
        wT = [sb(f"wT{n}", [P, 2, IT, O3], F16) for n in range(3)]
        woT = sb("woT", [P, 2, IT, D], F16)
        ternT = sb("ternT", [P, IT, D], F16)
        q_pack = [sb(f"q_pack{i}", [P, STEP_COLS], F16) for i in range(NBUF)]
        k_pack = [sb(f"k_pack{i}", [P, STEP_COLS], F16) for i in range(NBUF)]
        v_pack = [sb(f"v_pack{i}", [P, 512]) for i in range(NBUF)]
        probs = sb("probs", [P, PSLOTS, 512])
        sums = sb("sums", [P, 4, 512])
        qk_stage = [sb(f"qk_stage{i}", [P, 2, QK_TILES, BLK], F16) for i in range(2)]
        v_stage = [sb(f"v_stage{i}", [P, 2, D]) for i in range(2)]
        row_max = sb("row_max", [P, 2, 8])
        max_units = sb("max_units", [P, 2, 2, 8])
        units_of = sb("units_of", [P, 2, 8])
        shift = [sb(f"shift{h}", [16, 128], F16) for h in range(2)]
        shift_hi = sb("shift_hi", [16, 128], F16)
        shift_scale = sb("shift_scale", [16, 2])
        recips = sb("recips", [P, 128])
        attn = sb("attn", [P, 512])
        attn_n = sb("attn_n", [P, 512])
        ident = sb("ident", [P, P])
        ones = sb("ones", [P, P])
        sum_sel = sb("sum_sel", [P, 4, DH])
        spread_sel = sb("spread_sel", [P, 4, P])
        bias_col = sb("bias_col", [P, 3, QK_TILES])
        bias_v = sb("bias_v", [P, 3, D])
        sc = sb("sc", [P, 3, 16])
        fin = sb("fin", [P, 8])
        row_add = sb("row_add", [P, D])
        alpha = sb("alpha", [P, 1])
        stats = v_stage[1][:, 0, 0:96].rearrange("p (k c) -> p k c", c=6)
        mv = v_stage[1][:, 1, 0:32].rearrange("p (k c) -> p k c", c=2)
        rs = sb("rs", [P, B, 6, 16])
        prep2 = xT[2][:, :, :, :].rearrange("p a b c -> p (a b c)").bitcast(F32)
        prep1 = xT[1][:, :, :, :].rearrange("p a b c -> p (a b c)").bitcast(F32)
        win_n = [prep2[:, n * 1536:(n + 1) * 1536].rearrange("p (a d) -> p a d", a=6) for n in range(3)]
        wout_n = [prep2[:, 4608 + n * 512:4608 + (n + 1) * 512].rearrange("p (a d) -> p a d", a=2) for n in range(3)]
        w_eff1 = prep2[:, 6144:7680].rearrange("p (a o) -> p a o", a=2)
        tern_n = prep2[:, 7680:8192].rearrange("p (a d) -> p a d", a=2)
        win_t = [prep1[:, n * 1536:(n + 1) * 1536].rearrange("p (a o) -> p a o", a=2) for n in range(3)]
        w_sq = prep1[:, 4608:6144].rearrange("p (a o) -> p a o", a=2)
        b_row = prep1[:, 6144:6912]
        b_sq = prep1[:, 6912:7680]
        bout_bc = prep1[:, 7680:8192].rearrange("p (n a m) -> p n a m", n=2, a=2)
        w_eff = [None, w_eff1, win_t[0]]
        bin_row = [q_pack[n][:, :].bitcast(F32)[:, 0:O3] for n in range(3)]
        bin_col = sb("bin_col", [P, 3, QK_TILES])
        bout_col = sb("bout_col", [P, 3, IT])
        bout2_row = v_stage[0][:, 0, :]
        x_ln = [[probs[:, k // 2, k % 2 * D:(k % 2 + 1) * D] for k in range(16)],
                [(sums[:, k // 2, k % 2 * D:(k % 2 + 1) * D] if k < 8 else
                  v_pack[k // 2 - 4][:, k % 2 * D:(k % 2 + 1) * D]) for k in range(16)]]
        x_fin = [qk_stage[i // 2][:, i % 2, :, :].rearrange("p o r -> p (o r)").bitcast(F32)[:, 0:D] for i in range(4)]
        y_fin = [probs[:, i, D:2 * D] for i in range(4)]
        o_fin = [probs[:, 4 + i, 0:D] for i in range(4)]

        ps = ctx.enter_context(nc.psum_tensor("ps", [P, 8, 512], F32))
        T_BANK, T_BANKS, O_BANK, D_BANK = 2, 4, 6, 7
        QK_BANK, V_BANK = 2, 6
        LN_BANK = 6

        win_in = [sem(f"win_in{n}") for n in range(3)]
        small_in = sem("small_in")
        tern_in = sem("tern_in")
        consts_ready = sem("consts_ready")
        pool_chain = sem("pool_chain")
        dve_chain = sem("dve_chain")
        wt_turned = sem("wt_turned")
        wt_copied = sem("wt_copied")
        bout_spread = sem("bout_spread")
        fused = sem("fused")
        fused_copied = sem("fused_copied")
        biased = sem("biased")
        scaled = sem("scaled")
        w_halved = sem("w_halved")
        squared = sem("squared")
        sq_summed = sem("sq_summed")
        roots_wanted = sem("roots_wanted")
        roots = sem("roots")
        w_split = sem("w_split")
        last_ready = sem("last_ready")
        last_summed = sem("last_summed")
        last_turned = sem("last_turned")
        x_in = [sem(f"x_in{b}") for b in range(B)]
        ln_var = sem("ln_var")
        ln_root = sem("ln_root")
        ln_scale = sem("ln_scale")
        ln_applied = sem("ln_applied")
        ln_turned = sem("ln_turned")
        ln_hi = sem("ln_hi")
        ln_lo = sem("ln_lo")
        lin_done = sem("lin_done")
        qk_hi = sem("qk_hi")
        qk_lo = sem("qk_lo")
        v_out = sem("v_out")
        qk_stored = [sem(f"qk_stored{i}") for i in range(2)]
        v_stored = [sem(f"v_stored{i}") for i in range(2)]
        packed = [sem(f"packed{i}") for i in range(NBUF)]
        scored = sem("scored")
        maxed = sem("maxed")
        max_ready = sem("max_ready")
        turned = sem("turned")
        split_hi = sem("split_hi")
        shift_in = [sem(f"shift_in{h}") for h in range(2)]
        scored_t = sem("scored_t")
        exped = sem("exped")
        bursts = sem("bursts")
        summed = sem("summed")
        ones_done = sem("ones_done")
        recip_done = sem("recip_done")
        o_copied = sem("o_copied")
        spread = sem("spread")
        normed = sem("normed")
        x_hi = sem("x_hi")
        x_lo = sem("x_lo")
        xf_in = [sem(f"xf_in{i}") for i in range(4)]
        row_added = sem("row_added")
        fin_mm = sem("fin_mm")
        fin_y = sem("fin_y")
        fin_acc = sem("fin_acc")
        fin_o = sem("fin_o")
        stored = [sem(f"stored{i}") for i in range(4)]

        block = ctx.enter_context(nc.Block())

        steps = [lv.steps for lv in LEVELS]
        lin_blocks = [r // BLK for r in rows_of]
        GX, U2, SV, RT, RV, GW, SX, GQ, GXN, ESC, TMP, TMP2 = range(12)
        SMALL_DMAS = 12
        QK_STORES = 4 * 16
        all_sums = 8 + sum(lv.sums * lv.steps for lv in LEVELS)
        FIN_TILES = B * L // P
        FIN_TURN = 8

        g_base = [sum(steps[:n]) for n in range(4)]
        b_base = [sum(lin_blocks[:n]) for n in range(4)]
        u_base = [sum(m.units * m.steps for m in LEVELS[:n]) for n in range(4)]
        v_base = [sum(m.bursts * m.steps for m in LEVELS[:n]) for n in range(4)]
        d_base = [sum(m.sum_bursts * m.steps for m in LEVELS[:n]) for n in range(4)]
        r_base = [sum((m.units + 2) * m.steps for m in LEVELS[:n]) for n in range(4)]

        def packed_base(n, i):
            return sum(16 * per_step_dmas(m) * len(range(i, LEVELS[m].steps, NBUF)) for m in range(n))

        def per_step_dmas(n):
            return 5 if n == 0 else 3

        def first_block(n):
            items = [("L", g) for g in range(QK_TILES + 1)]
            if n:
                tail = LEVELS[n - 1].tokens(False, False, True)
                items[4:4] = tail[4:]
                items[2:2] = tail[2:4]
                items[1:1] = tail[:2]
            return items

        def middle_blocks(n, emit, eng, between, late):
            first, last = 2, lin_blocks[n] - 2
            if n == 0:
                for blk in range(first, last):
                    emit(blk, blk % 2)
                    if between:
                        between(blk - 1)
                return
            turns = (last - first) // 2 - 1
            with eng.Fori(0, turns) as i:
                for k in range(2):
                    emit(i * 2 + (first + k), k)
            if late:
                late(n)
            for blk in range(first + 2 * turns, last):
                emit(blk, blk % 2)

        def last_blocks(n):
            tokens = LEVELS[n].tokens(False, True, False)
            items, done = [], 0
            for g in range(2 * (QK_TILES + 1)):
                items.append(("L", g))
                upto = min(len(tokens), -(-len(tokens) * g // 8))
                items += tokens[done:upto]
                done = upto
            return items

        def slots(n, emit, eng):
            turns = (steps[n] - NBUF) // NBUF
            emit(0, 0)
            with eng.Fori(0, turns) as i:
                for u in range(NBUF):
                    emit(i * NBUF + (1 + u), (1 + u) % NBUF)
            for s in range(1 + NBUF * turns, steps[n]):
                emit(s, s % NBUF)

        def block_row(n, blk):
            return blk % B * LEVELS[0].in_rows + blk // B * BLK if n == 0 else blk * BLK

        def stores_before(n, k):
            return sum(len(range(k, lin_blocks[m], 2)) for m in range(n))

        def level(n, eng, block, tokens, middle=None, late=None, last=None, between=None):
            for what, j in first_block(n):
                if what == "L":
                    block(n, 0, 0, j)
                else:
                    tokens(n - 1, steps[n - 1], steps[n - 1] % NBUF, [(what, j)])

            def whole(blk, k):
                for g in range(QK_TILES + 1):
                    block(n, blk, k, g)

            whole(1, 1)
            if n == 0 and between:
                between(0)
            if middle:
                middle(n)
            middle_blocks(n, whole, eng, between, late)
            if last:
                last(n)
            for what, j in last_blocks(n):
                if what == "L":
                    blk = lin_blocks[n] - 2 + j // (QK_TILES + 1)
                    block(n, blk, blk % 2, j % (QK_TILES + 1))
                else:
                    tokens(n, -1, 3, [(what, j)])
            slots(n, lambda s, u: tokens(n, s, u, LEVELS[n].tokens(*parts(n, s))), eng)

        def parts(n, s):
            if not isinstance(s, int):
                return True, True, True
            return 0 <= s < steps[n], s + 1 < steps[n], s >= 1

        def src_row(lv, s, u):
            if lv.n == 0:
                return s * lv.stride
            if lv.n == 1:
                return (s - u % 2) * (lv.stride // 2) + (u % 2) * lv.in_rows
            return (s - u % 4) * (lv.stride // 4) + (u % 4 // 2) * lv.in_rows

        def dst_row(lv, s, u):
            if lv.n == 0:
                return s * lv.T
            if lv.n == 1:
                return (s - u % 2) * (lv.T // 2) + (u % 2) * L
            return (s - u % 4) * (lv.T // 4) + (u % 4 // 2) * L

        OUT_ROWS0 = LEVELS[1].in_rows

        def prob_slot(lv, u, unit):
            return (4 * (u % 2) + unit) if lv.n == 0 else unit % PSLOTS

        def out_slices(lv, s, u, hl):
            x = xT[(lv.n + 1) % 3] if lv.n < 2 else xT[1]
            r = dst_row(lv, s, u)
            if lv.n == 2:
                return [x[:, hl, u % 2, ds(r, 512)]], [attn_n[:, :]]
            if lv.n == 1:
                return [x[:, hl, :, ds(r, 256)]], [attn_n[:, :].rearrange("p (g q) -> p g q", g=2)]
            return ([x[:, hl, :, ds(r + b * OUT_ROWS0, 128)] for b in range(B)],
                    [attn_n[:, b * 256:(b + 1) * 256].rearrange("p (g q) -> p g q", g=2) for b in range(B)])

        def final_phase(eng, tile, tokens, early=lambda: None, late=lambda: None):
            def tail(*names):
                tokens(2, steps[2], 0, [(name, 0) for name in names])

            turns = FIN_TILES // FIN_TURN
            tail("W", "O")
            early()
            for k in range(FIN_TURN):
                tile(0, k)
            tail("E", "R")
            with eng.Fori(1, turns - 1) as i:
                for k in range(FIN_TURN):
                    tile(i, k)
            tail("N", "H")
            for k in range(FIN_TURN):
                if k == FIN_TURN - 4:
                    late()
                tile(turns - 1, k)

        @block.gpsimd
        def _(pool):
            chained = 0

            def link(ins):
                nonlocal chained
                chained += 1
                ins.then_inc(pool_chain, 1)
                pool.wait_ge(pool_chain, chained)

            link(pool.memset(ident[:, :], 0.0))
            link(pool.affine_select(out=ident[:, :], in_=ident[:, :], compare_op=ALU.not_equal, fill=1.0,
                                    base=0, pattern=[[-1, P]], channel_multiplier=1))
            link(pool.memset(ones[:, :], 1.0))
            pool.sem_inc(consts_ready, 1)
            link(pool.memset(sum_sel[:, :, :], 0.0))
            sel = sum_sel[:, :, :].rearrange("p a (b c) -> p a b c", b=4)
            link(pool.affine_select(out=sel, in_=sel, compare_op=ALU.not_equal, fill=1.0,
                                    base=0, pattern=[[1, 4], [-1, 4], [0, 8]], channel_multiplier=0))
            link(pool.memset(spread_sel[:, :, :], 0.0))
            sel = spread_sel[:, :, :].rearrange("p a (b c) -> p a b c", b=4)
            link(pool.affine_select(out=sel, in_=sel, compare_op=ALU.not_equal, fill=1.0,
                                    base=0, pattern=[[-8, 4], [-32, 4], [0, 32]], channel_multiplier=1))
            for i in range(NBUF):
                two = k_pack[i][SHIFT_ROW:SHIFT_ROW + 2, :]
                link(pool.memset(two, SHIFT_HI))
                link(pool.affine_select(out=two, in_=two, compare_op=ALU.not_equal, fill=SHIFT_LO,
                                        base=-1, pattern=[[0, STEP_COLS]], channel_multiplier=1))
            link(pool.memset(units_of[:, 0, :], -1.0 / SHIFT_HI))
            link(pool.memset(units_of[:, 1, :], -1.0 / SHIFT_LO))
            link(pool.memset(shift_scale[:, 0:1], SHIFT_LO / SHIFT_HI))
            link(pool.memset(shift_scale[:, 1:2], -SHIFT_HI / SHIFT_LO))
            link(pool.memset(shift_scale[0:8, 0:1], 1.0))
            link(pool.memset(shift_scale[0:8, 1:2], 0.0))
            pool.sem_inc(consts_ready, 1)

            pool.sem_inc(x_lo, 1)
            pool.sem_inc(summed, 8)

            for n in (1, 2):
                w = w_eff[n]
                pool.wait_ge(fused_copied, n)
                if n == 1:
                    pool.wait_ge(sq_summed, n)
                    for it in range(IT):
                        m = pool.tensor_tensor(w_sq[:, it, :], w[:, it, :], w[:, it, :], ALU.mult)
                    m.then_inc(squared, 1)
                    pool.wait_ge(squared, n + 1)
                pool.wait_ge(scaled, n)
                link(pool.tensor_scalar(w, w, sc[:, n, GW:GW + 1], None, ALU.mult))
                link(pool.tensor_copy(wT[n][:, 0, :, :], w))
                pool.tensor_tensor(wT[n][:, 1, :, :], w, wT[n][:, 0, :, :], ALU.subtract).then_inc(w_halved, 1)

            def low_half(lv, s, u):
                pool.wait_ge(x_hi, s + (g_base[lv.n] + 1))
                dst, src = out_slices(lv, s, u, 1)
                hi, _ = out_slices(lv, s, u, 0)
                for k, (d, h, a) in enumerate(zip(dst, hi, src)):
                    ins = pool.tensor_tensor(d, a, h, ALU.subtract)
                ins.then_inc(x_lo, 1)

            for lv in LEVELS:
                def emit(s, u, lv=lv, u0=u_base[lv.n], d0=d_base[lv.n]):
                    has_c, _, has_n = parts(lv.n, s)
                    for k, (unit, a, b, o) in enumerate(lv.sum_jobs()):
                        if has_n and lv.n == 2 and k == 4:
                            low_half(lv, s - 1, (u - 1) % NBUF)
                        if not has_c:
                            continue
                        if k % 4 == 0:
                            pool.wait_ge(ones_done, s * 2 + (d0 + 8 + k // 4 - (lv.n == 1)))
                        pool.wait_ge(exped, s * lv.units + (u0 + T_BANKS + unit + 1))
                        pool.tensor_tensor(sums[:, o[0], o[1]:o[1] + o[2]], probs[:, a[0] % PSLOTS, a[1]:a[1] + a[2]],
                                           probs[:, b[0] % PSLOTS, b[1]:b[1] + b[2]], ALU.add).then_inc(summed, 1)
                    if has_n and lv.n < 2:
                        low_half(lv, s - 1, (u - 1) % NBUF)
                slots(lv.n, emit, pool)
                if lv.n < 2:
                    low_half(lv, lv.steps - 1, (lv.steps - 1) % NBUF)

            def tile(i, k):
                j = k % 4
                pool.wait_ge(xf_in[j], i * (4 * FIN_TURN) + 16 * (k // 4 + 1))
                pool.wait_ge(fin_o, i * FIN_TURN + (k + 1))
                pool.tensor_tensor(y_fin[j], x_fin[j], row_add[:, :], ALU.add).then_inc(fin_y, 1)

            def y_free():
                pool.wait_ge(row_added, 1)
                pool.wait_ge(bursts, PSLOTS + v_base[3])
                pool.wait_ge(summed, all_sums)

            final_phase(pool, tile, lambda *_: None, early=y_free, late=lambda: low_half(LEVELS[2], steps[2] - 1, 3))

        @block.sync
        def _(sp):
            for k in range(2):
                sp.sem_inc(qk_stored[k], QK_STORES)
                sp.sem_inc(v_stored[k], 16)
            for j in range(4):
                sp.sem_inc(stored[j], 16)
            def weights(n):
                sp.dma_start(win_n[n], t[f"L0_attn_Win{n}"].rearrange("(a p) d -> p a d", p=P)).then_inc(win_in[n], 16)
                sp.dma_start(wout_n[n], t[f"L0_attn_Wout{n}"].rearrange("(a p) d -> p a d", p=P)).then_inc(win_in[n], 16)

            def row(name, w):
                return t[name].rearrange("(o n) -> o n", o=1).broadcast_to((P, w))

            weights(0)
            for n in range(3):
                sp.dma_start(bin_row[n], row(f"L0_attn_bin{n}", O3)).then_inc(small_in, 16)
            with nc.allow_non_contiguous_dma(reason="short bias columns"):
                for n in range(3):
                    sp.dma_start(bin_col[:, n, :], t[f"L0_attn_bin{n}"][0:QK_TILES * P].rearrange("(a p) -> p a", p=P)).then_inc(small_in, 16)
                    sp.dma_start(bout_col[:, n, :], t[f"L0_attn_bout{n}"].rearrange("(a p) -> p a", p=P)).then_inc(small_in, 16)
            sp.dma_start(bout2_row, row("L0_attn_bout2", D)).then_inc(small_in, 16)
            sp.dma_start(row_add[:, :], row("L0_ffn_bias", D)).then_inc(small_in, 16)
            sp.dma_start(alpha[:, :], row("L0_ffn_alpha", 1)).then_inc(small_in, 16)
            weights(1)
            sp.dma_start(probs[:, :, :].rearrange("p a (t d) -> p (a t) d", d=D),
                         x_d[0:L, :].rearrange("(a p) d -> p a d", p=P)).then_inc(x_in[0], 16)
            weights(2)
            sp.dma_start(sums[:, :, :].rearrange("p a (t d) -> p (a t) d", d=D),
                         x_d[L:L + 8 * P, :].rearrange("(a p) d -> p a d", p=P)).then_inc(x_in[1], 16)
            for i in range(NBUF):
                r = L + (8 + 2 * i) * P
                sp.dma_start(v_pack[i][:, :].rearrange("p (a d) -> p a d", d=D),
                             x_d[r:r + 2 * P, :].rearrange("(a p) d -> p a d", p=P)).then_inc(x_in[1], 16)
            sp.dma_start(tern_n, t["L0_ffn_weight"].rearrange("(a p) d -> p a d", p=P)).then_inc(tern_in, 16)

            def all_stored(n, blocks):
                for k in range(2):
                    count = stores_before(n, k) + len(range(k, blocks, 2)) + 1
                    sp.wait_ge(qk_stored[k], QK_STORES * count)
                    sp.wait_ge(v_stored[k], 16 * count)

            def block(n, blk, k, group):
                if group < QK_TILES:
                    return
                sp.wait_ge(qk_lo, blk * QK_TILES + (QK_TILES * (b_base[n] + 1) + QK_TILES))
                row = block_row(n, blk)
                dst = qk_d[n].rearrange("o p s r -> p o s r")
                for strip, half, o0, o1 in ((1, 0, 0, 4), (2, 1, 0, 4), (0, 0, 0, 2), (0, 1, 2, 4)):
                    sp.dma_start(dst[:, o0:o1, strip, ds(row, BLK)], qk_stage[k][:, half, o0:o1, :]).then_inc(qk_stored[k], 16)
                sp.wait_ge(v_out, blk + (b_base[n] + 2))
                sp.dma_start(v_d[n][ds(row, BLK), :].rearrange("(a p) d -> p a d", p=P), v_stage[k][:, :, :]).then_inc(v_stored[k], 16)

            def load(n, s, u):
                lv, i = LEVELS[n], u % NBUF
                past = s - (NBUF - 1)
                if isinstance(s, int):
                    past = max(past, 0)
                sp.wait_ge(bursts, past * lv.bursts + (v_base[n] + PSLOTS))
                r = src_row(lv, s, u)
                o0, on = (0, 2) if n < 2 else (u % 2, 1)
                for b in range(lv.batches):
                    row = r + b * lv.in_rows
                    c0, c1 = b * lv.heads * lv.T, (b + 1) * lv.heads * lv.T
                    for pack, tile0 in ((q_pack[i], 0), (k_pack[i], IT)):
                        src = qk_d[n][tile0 + o0:tile0 + o0 + on, :, :, ds(row, lv.T)]
                        sp.dma_start(pack[0:SHIFT_ROW, c0:c1].rearrange("p (h r) -> p h r", r=lv.T),
                                     src.rearrange("o (h p) s r -> (p s) (o h) r", p=DH)).then_inc(packed[i], 16)
                if n == 0:
                    src = v_d[n].rearrange("(b r) d -> r b d", b=B)[ds(r, P), :, :]
                elif n == 1:
                    src = v_d[n][ds(r, lv.T), :].rearrange("(a p) d -> p a d", p=P)
                else:
                    src = v_d[n][ds(r, lv.T), (u % 2) * P:(u % 2 + 1) * P].rearrange("(a p) d -> p a d", p=P)
                dst = v_pack[i][:, :].rearrange("p (a d) -> p a d", a=4 if n == 2 else 2)
                sp.dma_start(dst, src).then_inc(packed[i], 16)

            def tokens(n, s, u, todo):
                lv = LEVELS[n]
                if isinstance(s, int) and s == 0:
                    all_stored(n, lin_blocks[n])
                    if n == 2:
                        for j in range(4):
                            sp.dma_start(x_fin[j], x_d[j * P:(j + 1) * P, :]).then_inc(xf_in[j], 16)
                for what, h in todo:
                    if what == "M":
                        sp.wait_ge(maxed, s * (lv.units + 2) + (r_base[n] + lv.units + 2 + lv.ring("M", h) + 3))
                        sp.dma_start(q_pack[(u + 1) % NBUF][SHIFT_ROW:SHIFT_ROW + 2, h * 1024:(h + 1) * 1024],
                                     shift[h][:, :]).then_inc(shift_in[h], 16)
                        if h == LOAD_AFTER[n] and (not isinstance(s, int) or 0 <= s < lv.steps - 3):
                            load(n, s + 3, (u + 3) % NBUF)

            def first_loads(n):
                if n:
                    all_stored(n, (LEVELS[n].in_rows + 2 * BLK - 1) // BLK + (n == 2))
                    for s in range(1, NBUF - 1):
                        load(n, s, s)

            def first_load(n):
                all_stored(n, 2)
                load(n, 0, 0)

            def first_loads0(i):
                if i == 1:
                    all_stored(0, B)
                loads_after = (1, 3, 4)
                if i in loads_after:
                    step = loads_after.index(i)
                    load(0, step, step)

            for lv in LEVELS:
                level(lv.n, sp, block, tokens, late=first_load, last=first_loads, between=first_loads0)

            def load_next(tile, j):
                sp.wait_ge(fin_y, tile + (j + 1))
                sp.dma_start(x_fin[j % 4], x_d[ds(tile * P + (4 + j) * P, P), :]).then_inc(xf_in[j % 4], 16)

            def store(tile, j):
                sp.wait_ge(fin_o, tile + (j + 5))
                sp.dma_start(out_d[ds(tile * P + j * P, P), :], o_fin[j % 4]).then_inc(stored[j % 4], 16)

            turns = FIN_TILES // FIN_TURN
            with sp.Fori(0, turns - 1) as i:
                for j in range(FIN_TURN):
                    load_next(i * FIN_TURN, j)
                    store(i * FIN_TURN, j)
            for j in range(FIN_TURN):
                if j < FIN_TURN - 4:
                    load_next((turns - 1) * FIN_TURN, j)
                store((turns - 1) * FIN_TURN, j)
            for j in range(4):
                sp.wait_ge(stored[j], 16 * (FIN_TILES // 4 + 1))

        PRODUCTS = ((0, 0), (1, 0), (0, 1))

        @block.tensor
        def _(pe):
            pe.sem_inc(bursts, PSLOTS)
            pe.sem_inc(ones_done, 8)
            pe.wait_ge(consts_ready, 1)

            def turn_weights(n):
                pe.wait_ge(win_in[n], 32)
                if n:
                    pe.wait_ge(wt_copied, n)
                for it in range(IT):
                    for o in range(6):
                        m = pe.transpose(ps[:, 2 * it + o // 3, (o % 3) * P:(o % 3 + 1) * P],
                                         win_n[n][:, o, it * P:(it + 1) * P], ident[:, :])
                m.then_inc(wt_turned, 1)

            def squares(n):
                pe.wait_ge(squared, n + 1)
                if n:
                    pe.wait_ge(biased, n)
                for oh in range(2):
                    for jt in range(IT):
                        m = pe.matmul(ps[:, 4 + oh, 0:384], ones[:, :], w_sq[:, jt, oh * 384:(oh + 1) * 384],
                                      start=jt == 0, stop=jt == 1)
                m.then_inc(sq_summed, 1)

            def fuse(n):
                pe.wait_ge(roots_wanted, n)
                if n == 1:
                    pe.wait_ge(wt_copied, 3)
                else:
                    pe.wait_ge(fused_copied, n - 1)
                for it in range(IT):
                    for oh in range(2):
                        for jt in range(IT):
                            pe.matmul(ps[:, 2 * it + oh, 0:384], wout_n[n - 1][:, jt, it * P:(it + 1) * P],
                                      win_t[n][:, jt, oh * 384:(oh + 1) * 384], start=jt == 0, stop=jt == 1)
                pe.wait_ge(bout_spread, 1)
                for oh in range(2):
                    for jt in range(IT):
                        pe.matmul(ps[:, 4 + oh, 0:384], bout_bc[:, n - 1, jt, :],
                                  win_t[n][:, jt, oh * 384:(oh + 1) * 384], start=jt == 0, stop=jt == 1)
                for o in range(QK_TILES):
                    for jt in range(IT):
                        m = pe.matmul(ps[:, 5, 400 + o:401 + o], win_t[n][:, jt, o * P:(o + 1) * P],
                                      bout_col[:, n - 1, jt:jt + 1], start=jt == 0, stop=jt == 1)
                m.then_inc(fused, 1)

            def turn_rows(b):
                for q in range(8):
                    g = 8 * b + q
                    pe.wait_ge(ln_applied, 16 * b + 2 * q + 2)
                    pe.wait_ge(ln_lo, g + 1)
                    for a in range(2):
                        for it in range(IT):
                            m = pe.transpose(ps[:, LN_BANK + g % 2, it * 256 + a * P:it * 256 + (a + 1) * P],
                                             x_ln[b][2 * q + a][:, it * P:(it + 1) * P], ident[:, :])
                    m.then_inc(ln_turned, 1)

            turn_weights(0)
            turn_weights(1)
            squares(0)
            turn_weights(2)
            fuse(1)
            turn_rows(0)
            squares(1)
            fuse(2)
            turn_rows(1)
            squares(2)
            pe.wait_ge(w_split, 1)
            pe.wait_ge(roots_wanted, 3)
            pe.wait_ge(fused_copied, 2)
            pe.wait_ge(ln_lo, 16 + 2)
            pe.wait_ge(consts_ready, 2)

            def last_weights(i):
                if i == 1:
                    pe.wait_ge(last_ready, 1)
                    pe.matmul(ps[:, D_BANK, 0:2], ones[:, :], fin[:, 0:2], start=True, stop=True).then_inc(last_summed, 1)
                    for it in range(IT):
                        for a in range(2):
                            pe.transpose(ps[:, 0, it * D + a * P:it * D + (a + 1) * P],
                                         wout_n[2][:, a, it * P:(it + 1) * P], ident[:, :])
                if i == 2:
                    pe.wait_ge(last_ready, 2)
                    for it in range(IT):
                        for a in range(2):
                            m = pe.transpose(ps[:, 1, it * D + a * P:it * D + (a + 1) * P],
                                             tern_n[:, a, it * P:(it + 1) * P], ident[:, :])
                    m.then_inc(last_turned, 1)

            def block(n, blk, k, group):
                x, w, b0 = xT[n], wT[n], b_base[n]
                first = isinstance(blk, int) and blk == 0
                if n == 0:
                    col = blk % B * L + blk // B * BLK
                else:
                    col = blk * BLK
                if group < QK_TILES:
                    o = group
                    if first and group == 0 and n:
                        pe.wait_ge(x_lo, g_base[n] - 1)
                        pe.wait_ge(exped, u_base[n] + T_BANKS)
                        pe.wait_ge(w_halved, n)
                    pe.wait_ge(qk_lo, blk * QK_TILES + (QK_TILES * b0 + o + 1))
                    for it in range(IT):
                        for i, (wh, xh) in enumerate(PRODUCTS):
                            m = pe.matmul(ps[:, QK_BANK + o, 0:BLK], w[:, wh, it, o * P:(o + 1) * P], x[:, xh, it, ds(col, BLK)],
                                          start=it + i == 0, stop=it == 1 and i == 2)
                else:
                    if first:
                        pe.wait_ge(o_copied, g_base[n] + 1)
                    pe.wait_ge(v_out, blk + (b0 + 1))
                    for a in range(2):
                        for it in range(IT):
                            for i, (wh, xh) in enumerate(PRODUCTS):
                                m = pe.matmul(ps[:, V_BANK, a * D:(a + 1) * D], x[:, xh, it, ds(col + a * P, P)],
                                              w[:, wh, it, 2 * D:3 * D],
                                              start=it + i == 0, stop=it == 1 and i == 2)
                m.then_inc(lin_done, 1)

            def input_complete(n):
                if n:
                    pe.wait_ge(x_lo, g_base[n] + 1)

            def tokens(n, s, u, todo):
                lv, g0, u0, v0, r0 = LEVELS[n], g_base[n], u_base[n], v_base[n], r_base[n]
                at_start = isinstance(s, int) and s == 0
                qc, kc, vc = q_pack[u], k_pack[u], v_pack[u]
                qb, kb = q_pack[(u + 1) % NBUF], k_pack[(u + 1) % NBUF]
                ring0 = r0 + lv.units + 2
                for what, j in todo:
                    of, v_of, t_of = (s - 1, v_pack[u - 1], u - 1) if what in "WE" else (s, vc, u)
                    j = {"W": lv.bursts - 1, "E": lv.sum_bursts - 1}.get(what, j)
                    if what == "S":
                        bank = lv.ring("S", j)
                        if j == 0 and n == 0 and isinstance(s, int) and s < 0:
                            pe.wait_ge(w_split, 2)
                        if j == 0:
                            nb = (u + 1) % NBUF
                            pe.wait_ge(packed[nb], (s + 1 - nb) * (4 * per_step_dmas(n)) + (packed_base(n, nb) + 16 * per_step_dmas(n)))
                        pe.wait_ge(maxed, s * (lv.units + 2) + (ring0 + bank + 1))
                        for c, q, k, w_ in lv.query_unit(j):
                            m = pe.matmul(ps[:, bank % 2, c:c + w_], qb[0:SHIFT_ROW, q:q + P], kb[0:SHIFT_ROW, k:k + w_],
                                          start=True, stop=True)
                        m.then_inc(scored, 1)
                    elif what == "M":
                        bank = lv.ring("M", j)
                        pe.wait_ge(maxed, s * (lv.units + 2) + (ring0 + bank + 1))
                        pe.wait_ge(max_ready, s * 2 + (2 * g0 + 2 + j + 1))
                        pe.transpose(ps[0:16, bank % 2, 0:P], max_units[:, j, :, :].rearrange("p a c -> p (a c)"), ident[:, :]).then_inc(turned, 1)
                    elif what == "T":
                        if j == 0 or lv.shift_half(j) != lv.shift_half(j - 1):
                            pe.wait_ge(shift_in[lv.shift_half(j)], s * 16 + (16 * g0 + 16))
                        if j == 0 and at_start:
                            pe.wait_ge(qk_lo, QK_TILES * (b_base[n + 1] + 1))
                        pe.wait_ge(exped, s * lv.units + (u0 + j + 1))
                        for c, k, q, w_ in lv.key_unit(j):
                            m = pe.matmul(ps[:, T_BANK + j % T_BANKS, c:c + w_], kc[0:SHIFT_ROW + 2, k:k + P],
                                          qc[0:SHIFT_ROW + 2, q:q + w_], start=True, stop=True)
                        m.then_inc(scored_t, 1)
                    elif what in "VW":
                        pe.wait_ge(exped, of * lv.units + (u0 + (j + 1) * lv.per_burst + T_BANKS))
                        if j == 0 and at_start:
                            pe.wait_ge(v_out, b_base[n + 1] + 1)
                        if j == 0:
                            pe.wait_ge(o_copied, s + (g0 + 1))
                        for quad, unit, c, w_, vcol, oc, first, last in lv.value_products(j):
                            p = probs[:, prob_slot(lv, t_of, unit), c:c + w_]
                            m = pe.matmul(ps[quad * DH:(quad + 1) * DH, O_BANK, oc:oc + w_], v_of[:, vcol:vcol + DH], p,
                                          start=first, stop=last)
                        m.then_inc(bursts, 1)
                    elif what in "DE":
                        if lv.sums:
                            pe.wait_ge(summed, of * lv.sums + (lv.sums * (g0 - steps[0]) + 8 + 4 * (j + 1)))
                        if j == 0:
                            pe.wait_ge(normed, s + (g0 + 1))
                        for quad, buf, c, slab, first, last in lv.sum_products(j):
                            p = (sums[:, buf, c:c + P] if lv.sums else probs[:, prob_slot(lv, t_of, buf), c:c + P])
                            m = pe.matmul(ps[quad * DH:(quad + 1) * DH, D_BANK, 0:P], sum_sel[:, slab, :], p,
                                          start=first, stop=last)
                        m.then_inc(ones_done, 1)
                    elif what == "N":
                        pe.wait_ge(recip_done, s + g0)
                        for j4 in range(4):
                            m = pe.matmul(ps[:, D_BANK, j4 * P:(j4 + 1) * P], spread_sel[:, j4, :], recips[:, :],
                                          start=True, stop=True)
                        m.then_inc(spread, 1)
            for lv in LEVELS:
                level(lv.n, pe, block, tokens, middle=input_complete, between=last_weights)

            def tile(i, k):
                col, j = i * (FIN_TURN * P) + k * P, k % 4
                pe.wait_ge(fin_o, i * FIN_TURN + (k + 1))
                for it in range(IT):
                    for part, (wh, xh) in enumerate(PRODUCTS):
                        pe.matmul(ps[:, j, 0:D], xT[1][:, xh, it, ds(col, P)], woT[:, wh, it, :],
                                  start=it + part == 0, stop=it == 1 and part == 2)
                for it in range(IT):
                    for hl in range(2):
                        m = pe.matmul(ps[:, j, D:2 * D], xT[0][:, hl, it, ds(col, P)], ternT[:, it, :],
                                      start=it + hl == 0, stop=it + hl == 2)
                m.then_inc(fin_mm, 1)

            final_phase(pe, tile, tokens, early=lambda: pe.wait_ge(x_lo, g_base[3] - 1),
                        late=lambda: pe.wait_ge(x_lo, g_base[3] + 1))

        @block.scalar
        def _(act):
            act.sem_inc(exped, T_BANKS)
            act.sem_inc(o_copied, 1)
            def turned_out(n):
                act.wait_ge(wt_turned, n + 1)
                for it in range(IT):
                    for oh in range(2):
                        m = act.activation(win_t[n][:, it, oh * 384:(oh + 1) * 384], ps[:, 2 * it + oh, 0:384], ACT.Copy)
                m.then_inc(wt_copied, 1)

            def fused_out(n):
                act.wait_ge(fused, n)
                if n > 1:
                    act.wait_ge(w_split, 1)
                for it in range(IT):
                    for oh in range(2):
                        m = act.activation(w_eff[n][:, it, oh * 384:(oh + 1) * 384], ps[:, 2 * it + oh, 0:384], ACT.Copy)
                m.then_inc(fused_copied, 1)

            def bound_roots(n):
                act.wait_ge(roots_wanted, n + 1)
                act.activation(sc[:, n, RT:RT + 2], sc[:, n, U2:U2 + 2], ACT.Sqrt).then_inc(roots, 1)

            def ln_roots(b):
                act.wait_ge(ln_var, b + 1)
                act.activation(rs[:, b, 1, :], rs[:, b, 0, :], ACT.Sqrt).then_inc(ln_root, 1)

            def apply_ln(b, q):
                if q == 0:
                    act.wait_ge(ln_scale, b + 1)
                for k in (2 * q, 2 * q + 1):
                    act.activation(x_ln[b][k], x_ln[b][k], ACT.Identity, scale=rs[:, b, 4, k:k + 1],
                                   bias=rs[:, b, 5, k:k + 1]).then_inc(ln_applied, 1)

            def high_rows(b, q):
                g = 8 * b + q
                act.wait_ge(ln_turned, g + 1)
                act.activation(xT[0][:, 0, :, g * 256:(g + 1) * 256],
                               ps[:, LN_BANK + g % 2, :].rearrange("p (a r) -> p a r", a=IT), ACT.Copy).then_inc(ln_hi, 1)

            turned_out(0)
            turned_out(1)
            bound_roots(0)
            turned_out(2)
            ln_roots(0)
            for q in range(8):
                apply_ln(0, q)
            fused_out(1)
            for q in range(8):
                high_rows(0, q)
            bound_roots(1)
            ln_roots(1)
            for q in range(8):
                apply_ln(1, q)
            fused_out(2)
            for q in range(8):
                high_rows(1, q)
            bound_roots(2)

            def last_root(i):
                if i == 1:
                    act.wait_ge(roots_wanted, 4)
                    act.activation(fin[:, 3:4], fin[:, 2:3], ACT.Sqrt).then_inc(roots, 1)
                if i == 4:
                    act.wait_ge(w_halved, 2)

            def block(n, blk, k, group):
                if group == QK_TILES:
                    return
                if group == 0:
                    act.wait_ge(qk_stored[k], (blk - k) * (QK_STORES // 2) + QK_STORES * (stores_before(n, k) + 1))
                act.wait_ge(lin_done, blk * (QK_TILES + 1) + ((QK_TILES + 1) * b_base[n] + group + 1))
                act.activation(qk_stage[k][:, group // IT, group, :], ps[:, QK_BANK + group, 0:BLK], ACT.Identity,
                               bias=bias_col[:, n, group:group + 1]).then_inc(qk_hi, 1)

            def tokens(n, s, u, todo):
                lv, g0, u0, v0 = LEVELS[n], g_base[n], u_base[n], v_base[n]
                for what, j in todo:
                    if what == "T":
                        act.wait_ge(scored_t, s * lv.units + (u0 + j + 1))
                        if n == 0:
                            act.wait_ge(ones_done, s * lv.units + (j + 1))
                        else:
                            act.wait_ge(bursts, s * lv.bursts + (PSLOTS + v0 + j // 4 - 1))
                            k = j if n == 1 else 4 * (j // 8 + 1) + j % 4
                            act.wait_ge(summed, s * lv.sums + (lv.sums * (g0 - steps[0]) + k + 1))
                        act.activation(probs[:, prob_slot(lv, u, j), :], ps[:, T_BANK + j % T_BANKS, :], ACT.Exp,
                                       scale=sc[:, n, ESC:ESC + 1]).then_inc(exped, 1)
                    elif what == "O":
                        act.wait_ge(bursts, s * lv.bursts + (PSLOTS + v0))
                        act.wait_ge(normed, s + g0)
                        act.activation(attn[:, :], ps[:, O_BANK, :], ACT.Copy).then_inc(o_copied, 1)
                    elif what == "H":
                        act.wait_ge(normed, s + (g0 + 1))
                        dst, src = out_slices(lv, s - 1, (u - 1) % NBUF, 0)
                        for d, a in zip(dst, src):
                            m = act.activation(d, a, ACT.Copy)
                        m.then_inc(x_hi, 1)
            for lv in LEVELS:
                level(lv.n, act, block, tokens, between=last_root)
            tokens(2, steps[2], 0, [("O", 0), ("H", 0)])

        @block.vector
        def _(dve):
            chained = 0

            def link(ins):
                nonlocal chained
                chained += 1
                ins.then_inc(dve_chain, 1)
                dve.wait_ge(dve_chain, chained)

            def power_of_two(to, of, bound):
                link(dve.reciprocal(to, of))
                link(dve.tensor_scalar(to, to, bound, None, ALU.mult))
                link(dve.tensor_scalar(to.bitcast(I32), to.bitcast(I32), EXPONENT, None, ALU.bitwise_and))

            dve.sem_inc(maxed, 2)
            dve.sem_inc(normed, 1)
            dve.sem_inc(qk_lo, QK_TILES)
            dve.sem_inc(v_out, 1)
            dve.sem_inc(ln_lo, 2)
            dve.sem_inc(fin_o, 4)
            dve.wait_ge(consts_ready, 1)
            dve.wait_ge(small_in, 16 * SMALL_DMAS)

            def weights_of(n):
                return (win_t[0], bin_row[0], bin_col[:, 0, :]) if n == 0 else (w_eff[n], b_row, bin_col[:, n, :])

            def square(n):
                w, brow, bcol = weights_of(n)
                gx = sc[:, n, GX:GX + 1]
                if n == 0:
                    link(dve.memset(gx, 1.0))
                    dve.wait_ge(wt_copied, 1)
                else:
                    link(dve.tensor_copy(gx, sc[:, n - 1, GXN:GXN + 1]))
                    dve.wait_ge(fused, n)
                    for oh in range(2):
                        dve.tensor_tensor(b_row[:, oh * 384:(oh + 1) * 384], ps[:, 4 + oh, 0:384],
                                          bin_row[n][:, oh * 384:(oh + 1) * 384], ALU.add)
                    link(dve.tensor_tensor(bcol, ps[:, 5, 400:400 + QK_TILES], bcol, ALU.add))
                    dve.sem_inc(biased, 1)
                if n != 1:
                    if n:
                        dve.wait_ge(fused_copied, n)
                    for it in range(IT):
                        m = dve.tensor_tensor(w_sq[:, it, :], w[:, it, :], w[:, it, :], ALU.mult)
                    m.then_inc(squared, 1)
                link(dve.tensor_scalar(b_sq, brow, gx, None, ALU.mult))
                link(dve.tensor_tensor(b_sq, b_sq, b_sq, ALU.mult))

            def col_of(n):
                return lambda k, w=1: sc[:, n, k:k + w]

            def bounds(n):
                col = col_of(n)
                dve.wait_ge(sq_summed, n + 1)
                r2 = (NORM_BOUND if n == 0 else ROW_BOUND) ** 2
                dve.scalar_tensor_tensor(out=b_sq[:, 0:384], in0=ps[:, 4, 0:384], scalar=r2, in1=b_sq[:, 0:384],
                                         op0=ALU.mult, op1=ALU.add)
                link(dve.scalar_tensor_tensor(out=b_sq[:, 384:768], in0=ps[:, 5, 0:384], scalar=r2, in1=b_sq[:, 384:768],
                                              op0=ALU.mult, op1=ALU.add))
                dve.reduce_max(col(U2), b_sq, AX_X)
                link(dve.reduce_sum(col(SV), b_sq[:, 2 * D:3 * D], AX_X))
                dve.tensor_scalar(col(U2, 2), col(U2, 2), 2.0, 1e-30, ALU.mult, ALU.add).then_inc(roots_wanted, 1)

            def scale(n):
                w, brow, bcol = weights_of(n)
                col = col_of(n)
                dve.wait_ge(roots, n + 1)
                power_of_two(col(GW), col(RT), ACC_BOUND)
                link(dve.tensor_tensor(col(TMP), col(RV), col(GW), ALU.mult))
                power_of_two(col(SX), col(TMP), ROW_BOUND)
                link(dve.tensor_tensor(col(GQ), col(GX), col(GW), ALU.mult))
                dve.tensor_tensor(col(GXN), col(GQ), col(SX), ALU.mult)
                link(dve.tensor_tensor(col(TMP), col(GQ), col(GQ), ALU.mult))
                link(dve.reciprocal(col(TMP2), col(TMP)))
                dve.tensor_scalar(col(ESC), col(TMP2), float(DH) ** -0.5, None, ALU.mult)
                dve.tensor_scalar(bias_col[:, n, :], bcol, col(GQ), None, ALU.mult)
                dve.tensor_scalar(bias_v[:, n, :], brow[:, 2 * D:3 * D], col(GXN), None, ALU.mult)
                if n:
                    dve.sem_inc(scaled, 1)
                    return
                for it in range(IT):
                    m = dve.tensor_scalar(wT[0][:, 0, it, :], w[:, it, :], col(GW), None, ALU.mult)
                link(m)
                for it in range(IT):
                    m = dve.scalar_tensor_tensor(out=wT[0][:, 1, it, :], in0=w[:, it, :], scalar=col(GW),
                                                 in1=wT[0][:, 0, it, :], op0=ALU.mult, op1=ALU.subtract)
                m.then_inc(w_split, 1)

            def row_stats(b):
                dve.wait_ge(x_in[b], 16 * (1, 5)[b])
                for k in range(16):
                    m = dve.bn_stats(stats[:, k, :], x_ln[b][k])
                link(m)

            def row_scales(b):
                for k in range(16):
                    m = dve.bn_aggr(mv[:, k, :], stats[:, k, :])
                link(m)
                r = rs[:, b, :, :]
                dve.tensor_scalar(r[:, 0, :], mv[:, :, 1], EPS, None, ALU.add).then_inc(ln_var, 1)
                dve.wait_ge(ln_root, b + 1)
                link(dve.reciprocal(r[:, 2, :], r[:, 1, :]))
                link(dve.tensor_tensor(r[:, 3, :], r[:, 2, :], r[:, 2, :], ALU.mult))
                link(dve.tensor_tensor(r[:, 3, :], r[:, 3, :], r[:, 0, :], ALU.mult))
                link(dve.tensor_scalar(r[:, 3, :], r[:, 3, :], -0.5, 1.5, ALU.mult, ALU.add))
                link(dve.tensor_tensor(r[:, 4, :], r[:, 2, :], r[:, 3, :], ALU.mult))
                dve.scalar_tensor_tensor(out=r[:, 5, :], in0=mv[:, :, 0], scalar=-1.0, in1=r[:, 4, :],
                                         op0=ALU.mult, op1=ALU.mult).then_inc(ln_scale, 1)

            def low_rows(b):
                for g in range(8 * b, 8 * b + 8):
                    dve.wait_ge(ln_hi, g + 1)
                    dve.tensor_tensor(xT[0][:, 1, :, g * 256:(g + 1) * 256], ps[:, LN_BANK + g % 2, :].rearrange("p (a r) -> p a r", a=IT),
                                      xT[0][:, 0, :, g * 256:(g + 1) * 256], ALU.subtract).then_inc(ln_lo, 1)

            for n in range(2):
                for jt in range(IT):
                    m = dve.tensor_scalar(bout_bc[:, n, jt, :], ones[:, :], bout_col[:, n, jt:jt + 1], None, ALU.mult)
            m.then_inc(bout_spread, 1)
            square(0)
            row_stats(0)
            bounds(0)
            scale(0)
            row_scales(0)
            row_stats(1)
            square(1)
            low_rows(0)
            bounds(1)
            scale(1)
            row_scales(1)
            square(2)
            low_rows(1)
            bounds(2)
            link(dve.tensor_tensor(row_add[:, :], row_add[:, :], bout2_row, ALU.add))

            def last_weights(i):
                sq = w_sq[:, 0, 0:2 * D].rearrange("p (a d) -> p a d", a=2)
                if i == 0:
                    scale(2)
                    dve.wait_ge(tern_in, 16)
                    link(dve.tensor_tensor(w_sq[:, 0, 0:2 * D].rearrange("p (a d) -> p a d", a=2), wout_n[2], wout_n[2], ALU.mult))
                    dve.reduce_sum(fin[:, 0:1], w_sq[:, 0, 0:2 * D], AX_X)
                    dve.tensor_reduce(fin[:, 1:2], tern_n, mybir.AxisListType.XY, ALU.add, apply_absolute_value=True).then_inc(last_ready, 1)
                if i == 1:
                    dve.wait_ge(last_summed, 1)
                    dve.tensor_scalar(fin[:, 2:3], ps[:, D_BANK, 0:1], 1e-30, None, ALU.add).then_inc(roots_wanted, 1)
                    dve.tensor_scalar(fin[:, 4:5], ps[:, D_BANK, 1:2], 1.0 / (D * D), 0.7, ALU.mult, ALU.mult)
                    link(dve.tensor_scalar(fin[:, 5:6], ps[:, D_BANK, 1:2], 1.0 / (D * D), -0.7, ALU.mult, ALU.mult))
                    link(dve.tensor_scalar(sq, tern_n, fin[:, 5:6], None, ALU.is_lt))
                    link(dve.tensor_scalar(tern_n, tern_n, fin[:, 4:5], None, ALU.is_gt))
                    dve.tensor_tensor(tern_n, tern_n, sq, ALU.subtract).then_inc(last_ready, 1)
                    dve.wait_ge(roots, 4)
                    power_of_two(fin[:, 6:7], fin[:, 3:4], ACC_BOUND)
                    link(dve.tensor_tensor(fin[:, 7:8], fin[:, 6:7], sc[:, 2, GXN:GXN + 1], ALU.mult))
                    link(dve.reciprocal(fin[:, 7:8], fin[:, 7:8]))
                if i == 2:
                    dve.wait_ge(last_turned, 1)
                    wo = ps[:, 0, :].rearrange("p (a d) -> p a d", a=IT)
                    link(dve.tensor_scalar(woT[:, 0, :, :], wo, fin[:, 6:7], None, ALU.mult))
                    dve.scalar_tensor_tensor(out=woT[:, 1, :, :], in0=wo, scalar=fin[:, 6:7], in1=woT[:, 0, :, :],
                                             op0=ALU.mult, op1=ALU.subtract)
                    dve.tensor_copy(ternT[:, :, :], ps[:, 1, :].rearrange("p (a d) -> p a d", a=IT)).then_inc(w_split, 1)
                    dve.sem_inc(row_added, 1)

            def block(n, blk, k, group):
                if group == 0:
                    dve.wait_ge(qk_stored[k], (blk - k) * (QK_STORES // 2) + QK_STORES * (stores_before(n, k) + 1))
                if group < QK_TILES:
                    dve.wait_ge(qk_hi, blk * QK_TILES + (QK_TILES * b_base[n] + group + 1))
                    dve.scalar_tensor_tensor(out=qk_stage[k][:, 1 - group // IT, group, :], in0=ps[:, QK_BANK + group, 0:BLK],
                                             scalar=bias_col[:, n, group:group + 1], in1=qk_stage[k][:, group // IT, group, :],
                                             op0=ALU.add, op1=ALU.subtract).then_inc(qk_lo, 1)
                    return
                dve.wait_ge(v_stored[k], (blk - k) * 8 + 16 * (stores_before(n, k) + 1))
                dve.wait_ge(lin_done, blk * (QK_TILES + 1) + (QK_TILES + 1) * (b_base[n] + 1))
                for a in range(2):
                    m = dve.scalar_tensor_tensor(out=v_stage[k][:, a, :], in0=ps[:, V_BANK, a * D:(a + 1) * D],
                                                 scalar=sc[:, n, SX:SX + 1], in1=bias_v[:, n, :],
                                                 op0=ALU.mult, op1=ALU.add)
                m.then_inc(v_out, 1)

            def tokens(n, s, u, todo):
                lv, g0, u0, d0, r0 = LEVELS[n], g_base[n], u_base[n], d_base[n], r_base[n]
                for what, j in todo:
                    if what == "S":
                        dve.wait_ge(scored, s * lv.units + (u0 + lv.units + j + 1))
                        c = lv.mx_cols
                        h, c0 = j * c // 8, j * c % 8
                        dve.reduce_max(row_max[:, h, c0:c0 + c], ps[:, lv.ring("S", j) % 2, :].rearrange("p (a k) -> p a k", a=c),
                                       AX_X).then_inc(maxed, 1)
                        if c0 + c == 8:
                            dve.wait_ge(maxed, s * (lv.units + 2) + (r0 + lv.units + 2 + lv.last_scored(h) + 2))
                            dve.tensor_tensor(max_units[:, h, :, :], row_max[:, h, :].rearrange("p (o c) -> p o c", o=1).broadcast_to((P, 2, 8)),
                                              units_of[:, :, :], ALU.mult).then_inc(max_ready, 1)
                    elif what == "M":
                        big = ps[0:16, lv.ring("M", j) % 2, 0:P]
                        dve.wait_ge(turned, s * 2 + (2 * g0 + 2 + j + 1))
                        dve.tensor_scalar(shift_hi[:, :], big, shift_scale[:, 0:1], None, ALU.mult).then_inc(split_hi, 1)
                        dve.wait_ge(split_hi, s * 2 + (2 * g0 + 2 + j + 1))
                        if not isinstance(s, int) or s >= 0 or n:
                            dve.wait_ge(shift_in[j], s * 16 + (16 * g0 + 16))
                        dve.scalar_tensor_tensor(out=shift[j][:, :], in0=shift_hi[:, :], scalar=shift_scale[:, 1:2],
                                                 in1=big, op0=ALU.mult, op1=ALU.add).then_inc(maxed, 1)
                    elif what == "R":
                        dve.wait_ge(ones_done, s * lv.sum_bursts + (d0 + 8))
                        dve.reciprocal(recips[:, :], ps[:, D_BANK, 0:P]).then_inc(recip_done, 1)
                    elif what == "N":
                        dve.wait_ge(spread, s + g0)
                        dve.wait_ge(o_copied, s + (g0 + 1))
                        dve.wait_ge(x_lo, s + g0)
                        dve.tensor_tensor(attn_n[:, :], attn[:, :], ps[:, D_BANK, :], ALU.mult).then_inc(normed, 1)
            for lv in LEVELS:
                level(lv.n, dve, block, tokens, between=last_weights)

            def tile(i, k):
                j = k % 4
                dve.wait_ge(fin_mm, i * FIN_TURN + (k + 1))
                dve.wait_ge(fin_y, i * FIN_TURN + (k + 1))
                dve.scalar_tensor_tensor(out=y_fin[j], in0=ps[:, j, 0:D], scalar=fin[:, 7:8], in1=y_fin[j],
                                         op0=ALU.mult, op1=ALU.add).then_inc(fin_acc, 1)
                dve.wait_ge(fin_acc, i * FIN_TURN + (k + 1))
                dve.wait_ge(stored[j], i * (4 * FIN_TURN) + 16 * (k // 4 + 1))
                dve.scalar_tensor_tensor(out=o_fin[j], in0=ps[:, j, D:2 * D], scalar=alpha[:, 0:1], in1=y_fin[j],
                                         op0=ALU.mult, op1=ALU.add).then_inc(fin_o, 1)

            final_phase(dve, tile, tokens, early=lambda: dve.wait_ge(summed, all_sums))


_INS = (["L0_attn_x"] + [f"L0_attn_{w}{n}" for n in range(3) for w in ("Win", "bin", "Wout", "bout")]
        + ["L0_ffn_weight", "L0_ffn_alpha", "L0_ffn_bias"])


def kernel(**inputs):
    import numpy as _np
    import concourse.bacc as _bacc
    from concourse import mybir as _mybir
    from concourse.bass_utils import run_bass_kernel_spmd as _run

    nc = _bacc.Bacc("TRN2", target_bir_lowering=False, num_devices=1)
    arrays, handles = {}, {}
    for name in _INS:
        a = _np.ascontiguousarray(inputs[name])
        arrays[f"in_{name}"] = a
        handles[name] = nc.dram_tensor(f"in_{name}", a.shape, _mybir.dt.from_np(a.dtype), kind="ExternalInput").ap()
    out = nc.dram_tensor("out", (B, L, D), F32, kind="ExternalOutput").ap()
    build(nc, handles, out)
    r = _run(nc, [arrays], core_ids=[0])
    return r.results[0]["out"]
```
